# Optimizing a Trainium2 kernel written in Bass

```python
import numpy as np
import jax
import jax.numpy as jnp

def _softmax(x, axis=-1):
    return jax.nn.softmax(x, axis=axis)

def _gelu(x):
    return jax.nn.gelu(x, approximate=True)

def _silu(x):
    return jax.nn.silu(x)

def _sigmoid(x):
    return jax.nn.sigmoid(x)

def _layernorm(x, axis=-1, eps=1e-05):
    m = jnp.mean(x, axis=axis, keepdims=True)
    v = jnp.var(x, axis=axis, keepdims=True)
    return (x - m) / jnp.sqrt(v + eps)

def _scatter_add(tgt, idx, src, axis=0):
    return tgt.at[idx].add(src)

def _segment_sum(src, seg, n):
    return jax.ops.segment_sum(src, seg, n)
kernel_name = 'mk_prb_d1_jaxref_r8_3bb996'

def setup_inputs(seed: int=0):
    np.random.seed(seed)
    _w = jnp.asarray

    def _L0_attn_setup():
        import jax, jax.numpy as jnp
        import numpy as np
        H = 8
        LN_EPS = 1e-05
        key = jax.random.key(seed)
        ks = jax.random.split(key, 4)
        B, S, D = (4, 256, 128)
        x = jax.random.normal(ks[0], (B, S, D), dtype=jnp.float32)
        sc = 1.0 / np.sqrt(D)
        Wq = jax.random.normal(ks[1], (D, D), dtype=jnp.float32) * sc
        Wk = jax.random.normal(ks[2], (D, D), dtype=jnp.float32) * sc
        Wv = jax.random.normal(ks[3], (D, D * H), dtype=jnp.float32) * sc
        return {'x': x, 'Wq': Wq, 'bq': jnp.zeros((D,), jnp.float32), 'Wk': Wk, 'bk': jnp.zeros((D,), jnp.float32), 'Wv': Wv, 'bv': jnp.zeros((D * H,), jnp.float32), 'gamma': jnp.ones((D,), jnp.float32), 'beta': jnp.zeros((D,), jnp.float32)}
    _L0_attn_in = _L0_attn_setup()

    def _L0_ffn_setup():
        import jax, jax.numpy as jnp
        import numpy as np
        key = jax.random.key(seed)
        k_x, k_W, k_b, k_ids, k_w = jax.random.split(key, 5)
        N_ADAPTERS, D_OUT, D_IN = (32, 128, 128)
        B, S = (2, 256)
        K = 8
        x = jax.random.normal(k_x, (B, S, D_IN), dtype=jnp.float32)
        W = jax.random.normal(k_W, (N_ADAPTERS, D_OUT, D_IN), dtype=jnp.float32)
        b = jax.random.normal(k_b, (N_ADAPTERS, D_OUT), dtype=jnp.float32)
        ids = jax.random.randint(k_ids, (K,), 0, N_ADAPTERS, dtype=jnp.int64)
        weights = jax.random.uniform(k_w, (K,), dtype=jnp.float32)
        return {'x': x, 'W': W, 'b': b, 'ids': ids, 'weights': weights}
    _L0_ffn_in = _L0_ffn_setup()
    _d = {'L0_attn_x': _L0_attn_in['x'], 'L0_attn_Wq': _L0_attn_in['Wq'], 'L0_attn_bq': _L0_attn_in['bq'], 'L0_attn_Wk': _L0_attn_in['Wk'], 'L0_attn_bk': _L0_attn_in['bk'], 'L0_attn_Wv': _L0_attn_in['Wv'], 'L0_attn_bv': _L0_attn_in['bv'], 'L0_attn_gamma': _L0_attn_in['gamma'], 'L0_attn_beta': _L0_attn_in['beta'], 'L0_ffn_W': _L0_ffn_in['W'], 'L0_ffn_b': _L0_ffn_in['b'], 'L0_ffn_ids': _L0_ffn_in['ids'], 'L0_ffn_weights': _L0_ffn_in['weights']}
    _x0 = _d['L0_attn_x']
    _d['L0_attn_x'] = jax.random.normal(jax.random.fold_in(jax.random.key(seed), 1), (16, 256, 128), dtype=_x0.dtype)
    del _x0
    return _d

def reference(L0_attn_x, L0_attn_Wq, L0_attn_bq, L0_attn_Wk, L0_attn_bk, L0_attn_Wv, L0_attn_bv, L0_attn_gamma, L0_attn_beta, L0_ffn_W, L0_ffn_b, L0_ffn_ids, L0_ffn_weights):

    def _L0_attn_ref(x, Wq, bq, Wk, bk, Wv, bv, gamma, beta):
        import jax, jax.numpy as jnp
        import numpy as np
        H = 8
        LN_EPS = 1e-05
        B, S, D = x.shape
        dk = D // H
        mu = jnp.mean(x, axis=-1, keepdims=True)
        var = jnp.mean(jnp.square(x - mu), axis=-1, keepdims=True)
        xn = (x - mu) * jax.lax.rsqrt(var + LN_EPS) * gamma + beta
        q = (xn @ Wq + bq).reshape(B, S, H, dk).transpose(0, 2, 1, 3)
        k = (xn @ Wk + bk).reshape(B, S, H, dk).transpose(0, 2, 1, 3)
        v = (xn @ Wv + bv).reshape(B, S, H, D).transpose(0, 2, 1, 3)
        scores = jnp.einsum('bhsd,bhtd->bhst', q, k) / jnp.sqrt(jnp.asarray(dk, x.dtype))
        p = jax.nn.softmax(scores, axis=-1)
        att = jnp.einsum('bhst,bhtd->bhsd', p, v)
        out = att.reshape(S, B, D, H).sum(axis=-1).reshape(B, S, D)
        return out

    def _L0_ffn_ref(x, W, b, ids, weights):
        import jax, jax.numpy as jnp
        import numpy as np
        Wsel = W[ids]
        bsel = b[ids]
        out = jnp.einsum('k,kod,bsd->bso', weights, Wsel, x)
        out = out + jnp.einsum('k,ko->o', weights, bsel)
        return out
    x = L0_attn_x
    xn = _layernorm(x, axis=-1)
    x = x + _L0_attn_ref(xn, L0_attn_Wq, L0_attn_bq, L0_attn_Wk, L0_attn_bk, L0_attn_Wv, L0_attn_bv, L0_attn_gamma, L0_attn_beta) + _L0_ffn_ref(xn, L0_ffn_W, L0_ffn_b, L0_ffn_ids, L0_ffn_weights)
    return x

_drawn_inputs = setup_inputs


def setup_inputs(seed=0):
    import zlib

    import numpy as np

    out = dict(_drawn_inputs(seed))
    spreads = {'L0_attn_bq': (0.0, 0.8),
     'L0_attn_bk': (0.0, 0.8),
     'L0_attn_bv': (0.0, 0.493),
     'L0_attn_gamma': (1.0, 0.6),
     'L0_attn_beta': (0.0, 0.546)}
    factors = {}
    for name, (base, spread) in spreads.items():
        noise = np.random.default_rng([zlib.crc32(name.encode()), seed]).standard_normal(out[name].shape)
        drawn = base * np.exp(spread * noise) if base else spread * noise
        out[name] = jnp.asarray(drawn.astype(out[name].dtype))
    for name, factor in factors.items():
        out[name] = (out[name] * factor).astype(out[name].dtype)
    return out
```

```python
from contextlib import ExitStack

import concourse.bass as bass
from concourse import mybir

F32 = mybir.dt.float32
BF16 = mybir.dt.bfloat16
I32 = mybir.dt.int32
ALU = mybir.AluOpType
ACT = mybir.ActivationFunctionType
AX = mybir.AxisListType

P = 128
EPS = 1e-5
RING = 4
LEAD_PROJ, LEAD_STACK, LEAD_MAX, LEAD_ROWS = 4, 3, 2, 1


def build(nc, x, Wq, bq, Wk, bk, Wv, bv, gamma, beta, W, b, ids, weights, out):
    B, S, D = x.shape
    HG = Wv.shape[1]
    H = HG // D
    DK = D // H
    G = D // H
    K = ids.shape[0]
    N_AD = W.shape[0]
    TT = S // P
    NT = B * TT
    C = D // G
    A = S // C
    STACK = 6 * DK
    ROWS = STACK + 2
    HALF = H // 2
    SCALE = float(DK) ** -0.5
    assert D == P and A == 32 and G * C == D and HALF * A == P and B % RING == 0

    scratch = nc.dram_tensor("parts_dram", (RING, 6, P * S), BF16, kind="Internal").ap()
    x_tiles = x.rearrange("b (t p) d -> p (b t) d", p=P)
    out_tiles = out.rearrange("b (t p) d -> p (b t) d", p=P)

    with ExitStack() as ctx:
        def sb(name, shape, dt=F32):
            return ctx.enter_context(nc.sbuf_tensor(name, shape, dt))

        def ps(name, shape, dt=F32):
            return ctx.enter_context(nc.psum_tensor(name, shape, dt))

        def sem(name):
            return ctx.enter_context(nc.semaphore(name))

        x_flat = sb("x_flat", [P, NT * D])
        x_sb = x_flat[:, :].rearrange("p (n d) -> p n d", d=D)
        wq_sb, wk_sb = sb("wq_sb", [P, D]), sb("wk_sb", [P, D])
        wq_ord, wk_ord = sb("wq_ord", [P, D]), sb("wk_ord", [P, D])
        wqg, wkg = sb("wqg", [P, D]), sb("wkg", [P, D])
        wv_sb = sb("wv_sb", [P, HG])
        bv_sb = sb("bv_sb", [1, HG])
        wsel = sb("wsel", [P, K, D])
        bsel = sb("bsel", [K, D])
        ids_sb, ids_col = sb("ids_sb", [1, K], I32), sb("ids_col", [K, 1], I32)
        mix_all = sb("mix_all", [P, K])
        mix_col = sb("mix_col", [K, 1])
        mix_rows = sb("mix_rows", [K, P])
        gamma_col, beta_col = sb("gamma_col", [P, 1]), sb("beta_col", [P, 1])
        bq_col, bk_col = sb("bq_col", [P, 1]), sb("bk_col", [P, 1])
        bias_qk = sb("bias_qk", [P, 2])
        ones = sb("ones", [P, P])
        zeros = sb("zeros", [P, 2 * S])
        ident = sb("ident", [P, P])
        ident_bf = sb("ident_bf", [P, P], BF16)
        mix_ident = sb("mix_ident", [P, K, P])
        beta_bc = sb("beta_bc", [P, P])
        wv_sum = sb("wv_sum", [P, H * G])
        bv_sum = sb("bv_sum", [1, H * G])
        w_vy = sb("w_vy", [P, 2 * D])
        adapter_bias = sb("adapter_bias", [P, D])
        out_bias = sb("out_bias", [P, TT, D])
        bn = sb("bn", [P, NT, 6])
        mean_var = sb("mean_var", [P, NT * 2])
        var_in, std0, rstd0 = sb("var_in", [P, 2, NT]), sb("std0", [P, 2, NT]), sb("rstd0", [P, 2, NT])
        std, rstd = sb("std", [P, 2, NT]), sb("rstd", [P, 2, NT])
        rstd_flat = rstd[:, :, :].rearrange("p a n -> p (a n)")
        ratio = sb("ratio", [P, NT])
        z = sb("z", [P, RING, TT, D])
        zt_sb = sb("zt_sb", [P, RING, S])
        qk32 = sb("qk32", [P, 2, 2, S])
        rest = sb("rest", [P, 2, S])
        parts = sb("parts", [P, 2, 6, S], BF16)
        stack = sb("stack", [ROWS, RING, 2, H, S], BF16)
        nmax = sb("nmax", [P, 2, H * TT])
        nmax_parts = sb("nmax_parts", [P, 2, 2 * H * TT], BF16)
        nmax_rows = sb("nmax_rows", [2 * H * TT, 2, P], BF16)
        probs = sb("probs", [P, H, TT, S])
        values = sb("values", [P, RING, TT, H, 2 * G])
        adapters = sb("adapters", [P, RING, TT, D])
        att = sb("att", [P, 2, TT, C, 2 * G])
        rden = sb("rden", [P, 2, TT, C])
        normed = sb("normed", [P, 2, TT, D])
        summed = sb("summed", [P, 2, TT, D])
        result = sb("result", [P, 2, TT, D])

        max_ps = [ps(f"max_ps{i}", [P, TT, S]) for i in range(2)]
        exp_ps = [ps(f"exp_ps{i}", [P, TT, S]) for i in range(2)]
        out_ps = ps("out_ps", [P, 2 * S])
        zt_ps = ps("zt_ps", [P, 2 * S])
        qk_ps = ps("qk_ps", [P, 2, S])
        vy_ps = ps("vy_ps", [P, TT, 2 * D])
        nmax_ps = zt_ps[:, S:2 * S].bitcast(BF16)
        bias_ps = exp_ps[0][:, 0, 0:2]
        vbias_ps = exp_ps[0][:, 0, P:2 * P]
        abias_ps = exp_ps[0][:, 1, 0:P]
        adapt_ps = exp_ps[1][:, 0, 0:P]

        x_first, x_second, x_third = sem("x_first"), sem("x_second"), sem("x_third")
        ids_loaded, qk_loaded, v_loaded = sem("ids_loaded"), sem("qk_loaded"), sem("v_loaded")
        mix_loaded, adapters_loaded, abias_loaded = sem("mix_loaded"), sem("adapters_loaded"), sem("abias_loaded")
        ident_ready, pool_setup, dve_setup = sem("ident_ready"), sem("pool_setup"), sem("dve_setup")
        var_ready, std_ready, wqk_ready, bias_ready = sem("var_ready"), sem("std_ready"), sem("wqk_ready"), sem("bias_ready")
        bias_in_psum, vbias_ready, mix_ready = sem("bias_in_psum"), sem("vbias_ready"), sem("mix_ready")
        mixed_in_psum, consts_ready = sem("mixed_in_psum"), sem("consts_ready")
        z_ready, zt_in_psum, zt_in_sbuf = sem("z_ready"), sem("zt_in_psum"), sem("zt_in_sbuf")
        qk_in_psum, qk_in_sbuf = sem("qk_in_psum"), sem("qk_in_sbuf")
        split_steps, parts_stored = sem("split_steps"), sem("parts_stored")
        stack_loaded = [sem(f"stack_loaded{i}") for i in range(RING)]
        rows_loaded = [sem(f"rows_loaded{i}") for i in range(RING)]
        max_scores, max_done, nmax_split = sem("max_scores"), sem("max_done"), sem("nmax_split")
        nmax_in_psum, nmax_in_sbuf = sem("nmax_in_psum"), sem("nmax_in_sbuf")
        exp_scores, exp_done, out_in_psum = sem("exp_scores"), sem("exp_done"), sem("out_in_psum")
        vy_in_psum, values_ready, adapters_ready = sem("vy_in_psum"), sem("values_ready"), sem("adapters_ready")
        att_ready, rden_ready, normed_ready = sem("att_ready"), sem("rden_ready"), sem("normed_ready")
        final_steps = sem("final_steps")
        stored = [sem(f"stored{i}") for i in range(2)]

        def steps(engine, step, before=()):
            def one(t, base):
                step(lambda lead: base + (t + lead), lambda lead: (t + lead) % RING,
                     lambda lead: not isinstance(base, int) or 0 <= t + lead < B)

            for t in range(-LEAD_PROJ, 0):
                for work in [w for at, w in before if at == t]:
                    work()
                one(t, 0)
            with engine.Fori(0, (B - LEAD_PROJ) // RING) as i:
                for t in range(RING):
                    one(t, i * RING)
            for t in range(B - LEAD_PROJ, B):
                one(t, 0)

        START = 16
        started = [out_in_psum, final_steps, exp_scores, exp_done, att_ready, *stack_loaded, *rows_loaded, *stored]

        def release(engine, semaphore, value, start=0):
            if not isinstance(value, int) or value > 0:
                engine.wait_ge(semaphore, value + start)

        STATS = [(0, TT), (TT, 4 * TT), (4 * TT, NT)]
        LOADS = 6

        def stack_count(n, s, more):
            return (n - s) * (LOADS * 16 // RING) + more * 16

        block = ctx.enter_context(nc.Block())

        @block.sync
        def _(sp):
            sp.dma_start(x_sb[:, 0:TT, :], x_tiles[:, 0:TT, :]).then_inc(x_first, 16)
            sp.dma_start(x_sb[:, TT:4 * TT, :], x_tiles[:, TT:4 * TT, :]).then_inc(x_second, 16)
            sp.dma_start(wv_sb[:, :], Wv).then_inc(v_loaded, 16)
            sp.dma_start(bv_sb[:, :], bv.rearrange("(a n) -> a n", a=1)).then_inc(v_loaded, 16)
            sp.dma_start(x_sb[:, 4 * TT:NT, :], x_tiles[:, 4 * TT:NT, :]).then_inc(x_third, 16)

            sp.wait_ge(ids_loaded, 32)
            for k in range(K):
                which = sp.value_load(ids_sb[0:1, k:k + 1], min_val=0, max_val=N_AD - 1)
                sp.dma_start(wsel[:, k, :], W[bass.ds(which, 1)].rearrange("n o i -> o (n i)"))\
                  .then_inc(adapters_loaded, 16)

            def step(batch, slot, runs):
                if runs(LEAD_STACK):
                    n, s = batch(LEAD_STACK), slot(LEAD_STACK)
                    release(sp, stack_loaded[s], stack_count(n, s, 0), START)
                    sp.wait_ge(split_steps, n * 4 + 4)
                    sp.dma_start(scratch[s].rearrange("r (p s) -> p r s", p=P), parts[:, s % 2, :, :])\
                      .then_inc(parts_stored, 16)
                if runs(LEAD_ROWS):
                    n, s = batch(LEAD_ROWS), slot(LEAD_ROWS)
                    sp.wait_ge(nmax_in_sbuf, n + 1)
                    sp.dma_start(stack[STACK:ROWS, s, 0, :, :].rearrange("r h s -> r (h s)"),
                                 nmax_rows[:, s % 2, :]).then_inc(rows_loaded[s], 16)
                if runs(LEAD_STACK):
                    n, s = batch(LEAD_STACK), slot(LEAD_STACK)
                    release(sp, exp_scores, (n - RING + 1) * H, START)
                    sp.wait_ge(parts_stored, n * 16 + 16)
                    row = 0
                    for count in (3, 2, 1):
                        for side, first in ((0, 3 - count), (1, 3)):
                            sp.dma_start(stack[row:row + count * DK, s, side, :, :].rearrange("r h s -> r (h s)"),
                                         scratch[s, first:first + count, :].rearrange("r (k n) -> (r k) n", k=DK))\
                              .then_inc(stack_loaded[s], 16)
                        row += count * DK
                if runs(0):
                    n, s = batch(0), slot(0)
                    sp.wait_ge(final_steps, n * 2 + 2 + START)
                    sp.dma_start(out_tiles[:, bass.ds(n * TT, TT), :], result[:, s % 2, :, :])\
                      .then_inc(stored[s % 2], 16)

            steps(sp, step)
            for q in stored:
                sp.wait_ge(q, 16 * B // 2 + START)

        @block.gpsimd
        def _(pool):
            pool.memset(ident[:, :], 0.0).then_inc(pool_setup, 1)
            pool.memset(zeros[:, :], 0.0).then_inc(pool_setup, 1)
            pool.wait_ge(pool_setup, 2)
            pool.affine_select(out=ident[:, :], in_=ident[:, :], compare_op=ALU.not_equal, fill=1.0, base=0,
                               pattern=[[-1, P]], channel_multiplier=1).then_inc(ident_ready, 1)
            pool.wait_ge(ident_ready, 1)
            pool.tensor_tensor(ident_bf[:, :], ident[:, :], zeros[:, 0:P], ALU.add).then_inc(ident_ready, 1)

            pool.wait_ge(ids_loaded, 32)
            pool.indirect_dma_start(bsel[:, :], None, b, bass.IndirectOffsetOnAxis(ap=ids_col[:, 0:1], axis=0))\
                .then_inc(abias_loaded, 16)

            def constants():
                pool.memset(values[:, :, :, :, G:2 * G], 1.0).then_inc(pool_setup, 1)
                for s in range(RING):
                    pool.wait_ge(pool_setup, 3 + s)
                    pool.memset(stack[STACK:ROWS, s, 1, :, :], 1.0).then_inc(pool_setup, 1)
                pool.wait_ge(pool_setup, 3 + RING)

            def step(batch, slot, runs):
                if runs(LEAD_ROWS):
                    n, s = batch(LEAD_ROWS), slot(LEAD_ROWS)
                    nmax_n = nmax[:, s % 2, :]
                    high, low = nmax_parts[:, s % 2, 0:H * TT], nmax_parts[:, s % 2, H * TT:2 * H * TT]
                    pool.wait_ge(max_done, n * H + H)
                    release(pool, nmax_in_psum, n - 1)
                    pool.tensor_tensor(high, nmax_n, zeros[:, 0:H * TT], ALU.add).then_inc(nmax_split, 1)
                    pool.wait_ge(nmax_split, n * 2 + 1)
                    pool.tensor_tensor(low, nmax_n, high, ALU.subtract).then_inc(nmax_split, 1)
                if runs(LEAD_PROJ):
                    n, s = batch(LEAD_PROJ), slot(LEAD_PROJ)
                    qk_n, none = qk32[:, s % 2, :, :], zeros[:, :].rearrange("p (a s) -> p a s", a=2)
                    low, middle, high = parts[:, s % 2, 0:6:5, :], parts[:, s % 2, 1:5:3, :], parts[:, s % 2, 2:4, :]
                    pool.wait_ge(qk_in_sbuf, n * 2 + 2)
                    release(pool, parts_stored, (n - 1) * 16)
                    pool.tensor_tensor(high, qk_n, none, ALU.add).then_inc(split_steps, 1)
                    pool.wait_ge(split_steps, n * 4 + 1)
                    pool.tensor_tensor(rest[:, :, :], qk_n, high, ALU.subtract).then_inc(split_steps, 1)
                    pool.wait_ge(split_steps, n * 4 + 2)
                    pool.tensor_tensor(middle, rest[:, :, :], none, ALU.add).then_inc(split_steps, 1)
                    pool.wait_ge(split_steps, n * 4 + 3)
                    pool.tensor_tensor(low, rest[:, :, :], middle, ALU.subtract).then_inc(split_steps, 1)
                if runs(0):
                    n, s = batch(0), slot(0)
                    summed_n = summed[:, s % 2, :, :].rearrange("p t d -> p (t d)")
                    pool.wait_ge(adapters_ready, n * TT + TT)
                    pool.wait_ge(normed_ready, n + 1)
                    pool.tensor_tensor(summed_n, normed[:, s % 2, :, :].rearrange("p t d -> p (t d)"),
                                       adapters[:, s, :, :].rearrange("p t d -> p (t d)"), ALU.add)\
                        .then_inc(final_steps, 1)
                    pool.wait_ge(final_steps, n * 2 + 1 + START)
                    release(pool, stored[s % 2], (n - s % 2) * 8, START)
                    pool.tensor_tensor(result[:, s % 2, :, :].rearrange("p t d -> p (t d)"), summed_n,
                                       x_flat[:, bass.ds(n * TT * D, TT * D)], ALU.add).then_inc(final_steps, 1)

            steps(pool, step, before=[(-LEAD_PROJ + 1, constants)])

        @block.scalar
        def _(act):
            act.dma_start(wq_sb[:, :], Wq).then_inc(qk_loaded, 16)
            act.dma_start(wk_sb[:, :], Wk).then_inc(qk_loaded, 16)
            act.dma_start(gamma_col[:, :], gamma.rearrange("(p a) -> p a", a=1)).then_inc(qk_loaded, 16)
            act.dma_start(beta_col[:, :], beta.rearrange("(p a) -> p a", a=1)).then_inc(qk_loaded, 16)
            act.dma_start(ids_sb[:, :], ids.rearrange("(a k) -> a k", a=1)).then_inc(ids_loaded, 16)
            act.dma_start(ids_col[:, :], ids.rearrange("(k a) -> k a", a=1)).then_inc(ids_loaded, 16)
            act.dma_start(mix_col[:, :], weights.rearrange("(k a) -> k a", a=1)).then_inc(mix_loaded, 16)
            act.dma_start(mix_all[:, :], weights.rearrange("(a k) -> a k", a=1).to_broadcast([P, K]))\
               .then_inc(mix_loaded, 16)
            with nc.allow_non_contiguous_dma(reason="two vectors of 128 numbers, reordered"):
                for bias, col in ((bq, bq_col), (bk, bk_col)):
                    act.dma_start(col[:, :], bias.rearrange("(h k a) -> k h a", k=DK, a=1)).then_inc(qk_loaded, 16)

            def roots(group):
                def work():
                    lo, hi = STATS[group]
                    act.wait_ge(var_ready, 2 * group + 2)
                    nc.scalar.activation(std0[:, :, lo:hi], var_in[:, :, lo:hi], ACT.Sqrt).then_inc(std_ready, 1)
                return work

            def step(batch, slot, runs):
                for u in range(H):
                    if runs(0):
                        n = batch(0)
                        act.wait_ge(exp_scores, n * H + u + 1 + START)
                        if u % HALF == 0:
                            release(act, out_in_psum, n * 2 + (u // HALF - 1), START)
                        nc.scalar.activation(probs[:, u, :, :], exp_ps[u % 2][:, :, :], ACT.Exp, scale=SCALE)\
                          .then_inc(exp_done, 1)
                    if u == 1 and runs(LEAD_PROJ):
                        n, s = batch(LEAD_PROJ), slot(LEAD_PROJ)
                        act.wait_ge(zt_in_psum, n + 1)
                        release(act, vy_in_psum, n - RING + 1)
                        nc.scalar.activation(zt_sb[:, s, :], zt_ps[:, 0:S], ACT.Copy).then_inc(zt_in_sbuf, 1)
                    if u == 3 and runs(LEAD_ROWS):
                        n, s = batch(LEAD_ROWS), slot(LEAD_ROWS)
                        act.wait_ge(nmax_in_psum, n + 1)
                        if not isinstance(n, int) or n >= 2:
                            act.wait_ge(rows_loaded[(s - 2) % RING], n * (16 // RING) + (16 - (2 + (s - 2) % RING) * (16 // RING) + START))
                        nc.scalar.activation(nmax_rows[:, s % 2, :], nmax_ps[0:2 * H * TT, 0:P], ACT.Copy)\
                          .then_inc(nmax_in_sbuf, 1)
                    if u == 4 and runs(LEAD_PROJ):
                        n, s = batch(LEAD_PROJ), slot(LEAD_PROJ)
                        act.wait_ge(qk_in_psum, n + 1)
                        release(act, split_steps, (n - 2) * 4 + 2)
                        if isinstance(n, int) and n == 0:
                            act.wait_ge(bias_ready, 1)
                        for side in range(2):
                            nc.scalar.activation(qk32[:, s % 2, side, :], qk_ps[:, side, :], ACT.Identity,
                                                 bias=bias_qk[:, side:side + 1]).then_inc(qk_in_sbuf, 1)
                if runs(LEAD_ROWS):
                    n, s = batch(LEAD_ROWS), slot(LEAD_ROWS)
                    act.wait_ge(vy_in_psum, n + 1)
                    release(act, out_in_psum, n * 2 - 2 * (RING - 1), START)
                    for t in range(TT):
                        last = nc.scalar.activation(values[:, s, t, :, 0:G],
                                                    vy_ps[:, t, 0:D].rearrange("p (h g) -> p h g", g=G), ACT.Copy)
                    last.then_inc(values_ready, 1)

            steps(act, step, before=[(-LEAD_PROJ + k, roots(k)) for k in range(len(STATS))])

        @block.vector
        def _(dve):
            done = [0]

            def link(ins):
                done[0] += 1
                ins.then_inc(dve_setup, 1)
                dve.wait_ge(dve_setup, done[0])

            mv = mean_var[:, :].rearrange("p (n a) -> p n a", a=2)

            def statistics(group):
                lo, hi = STATS[group]
                dve.wait_ge((x_first, x_second, x_third)[group], 16)
                for n in range(lo, hi):
                    last = nc.vector.bn_stats(bn[:, n, :], x_sb[:, n, :])
                link(last)
                for n in range(lo, hi):
                    last = nc.vector.bn_aggr(mv[:, n, :], bn[:, n, :])
                link(last)
                nc.vector.tensor_scalar(var_in[:, 0, lo:hi], mv[:, lo:hi, 1], EPS, None, ALU.add).then_inc(var_ready, 1)
                nc.vector.tensor_scalar(var_in[:, 1, lo:hi], mv[:, lo:hi, 1], 1.0 + EPS, EPS * EPS,
                                        ALU.mult, ALU.add).then_inc(var_ready, 1)

            def deviations(group):
                lo, hi = STATS[group]
                v, s0, r0 = var_in[:, :, lo:hi], std0[:, :, lo:hi], rstd0[:, :, lo:hi]
                s1, r1 = std[:, :, lo:hi], rstd[:, :, lo:hi]
                dve.wait_ge(std_ready, group + 1)
                link(nc.vector.reciprocal(r0, s0))
                link(nc.vector.tensor_tensor(s1, v, r0, ALU.mult))
                link(nc.vector.tensor_tensor(s1, s1, s0, ALU.add))
                link(nc.vector.tensor_scalar(s1, s1, 0.5, None, ALU.mult))
                link(nc.vector.reciprocal(r1, s1))
                link(nc.vector.tensor_tensor(ratio[:, lo:hi], std[:, 1, lo:hi], rstd[:, 0, lo:hi], ALU.mult))

            def first():
                nc.vector.memset(ones[:, :], 1.0)
                statistics(0)
                dve.wait_ge(qk_loaded, 16 * 6)
                for w, ordered, scaled in ((wq_sb, wq_ord, wqg), (wk_sb, wk_ord, wkg)):
                    by_column = w[:, :].rearrange("p (h k) -> p k h", k=DK)
                    nc.vector.tensor_copy(ordered[:, :].rearrange("p (k h) -> p k h", k=DK), by_column)
                    nc.vector.tensor_scalar(scaled[:, :].rearrange("p (k h) -> p k h", k=DK), by_column,
                                            gamma_col[:, :], None, ALU.mult).then_inc(wqk_ready, 1)
                deviations(0)

            def second():
                dve.wait_ge(bias_in_psum, 1)
                nc.vector.tensor_tensor(bias_qk[:, 0:1], bias_ps[:, 0:1], bq_col[:, :], ALU.add)
                nc.vector.tensor_tensor(bias_qk[:, 1:2], bias_ps[:, 1:2], bk_col[:, :], ALU.add).then_inc(bias_ready, 1)
                statistics(1)
                deviations(1)

            def third():
                statistics(2)
                dve.wait_ge(v_loaded, 32)
                link(nc.vector.tensor_reduce(wv_sum[:, :], wv_sb[:, :].rearrange("p (n j) -> p n j", j=H), AX.X, ALU.add))
                nc.vector.tensor_reduce(bv_sum[:, :], bv_sb[:, :].rearrange("p (n j) -> p n j", j=H), AX.X, ALU.add)
                nc.vector.tensor_scalar(w_vy[:, 0:D], wv_sum[:, :], gamma_col[:, :], None, ALU.mult)
                nc.vector.tensor_scalar(beta_bc[:, :], ones[:, :], beta_col[:, :], None, ALU.mult)
                dve.wait_ge(mix_loaded, 32)
                dve.wait_ge(ident_ready, 1)
                nc.vector.tensor_scalar(mix_rows[:, :], ones[0:K, :], mix_col[:, :], None, ALU.mult).then_inc(vbias_ready, 1)
                for k in range(K):
                    last = nc.vector.tensor_scalar(mix_ident[:, k, :], ident[:, :], mix_all[:, k:k + 1], None, ALU.mult)
                last.then_inc(mix_ready, 1)
                deviations(2)
                dve.wait_ge(mixed_in_psum, 1)
                nc.vector.tensor_copy(w_vy[:, D:2 * D], adapt_ps)
                link(nc.vector.tensor_copy(adapter_bias[:, :], abias_ps))
                for t in range(TT):
                    for j in range(HALF):
                        q = slice(A * j, A * j + A)
                        head = (t * HALF + j) * G
                        last = nc.vector.tensor_tensor(
                            out_bias[q, t, :].rearrange("p (c g) -> p c g", g=G),
                            vbias_ps[q, head:head + G].rearrange("p (a g) -> p a g", a=1).to_broadcast([A, C, G]),
                            adapter_bias[q, :].rearrange("p (c g) -> p c g", g=G), ALU.add)
                last.then_inc(consts_ready, 1)

            def step(batch, slot, runs):
                if runs(LEAD_PROJ):
                    n, s = batch(LEAD_PROJ), slot(LEAD_PROJ)
                    release(dve, zt_in_psum, n - RING + 1)
                    for t in range(TT):
                        tile = n * TT + t
                        nc.vector.tensor_scalar(z[:, s, t, :], x_flat[:, bass.ds(tile * D, D)],
                                                mean_var[:, bass.ds(tile * 2, 1)], rstd_flat[:, bass.ds(tile + NT, 1)],
                                                ALU.subtract, ALU.mult).then_inc(z_ready, 1)
                if runs(LEAD_MAX):
                    n, s = batch(LEAD_MAX), slot(LEAD_MAX)
                    release(dve, nmax_split, (n - 1) * 2)
                    for u in range(H):
                        dve.wait_ge(max_scores, n * H + u + 1)
                        nc.vector.tensor_reduce(nmax[:, s % 2, u * TT:(u + 1) * TT], max_ps[u % 2][:, :, :], AX.X,
                                                ALU.max, negate=True).then_inc(max_done, 1)
                if runs(LEAD_ROWS):
                    n, s = batch(LEAD_ROWS), slot(LEAD_ROWS)
                    dve.wait_ge(values_ready, n + 1)
                    release(dve, final_steps, n * 2 - 2 * (RING - 1), START)
                    for t in range(TT):
                        nc.vector.scalar_tensor_tensor(adapters[:, s, t, :], vy_ps[:, t, D:2 * D],
                                                       ratio[:, bass.ds(n * TT + t, 1)], out_bias[:, t, :],
                                                       ALU.mult, ALU.add).then_inc(adapters_ready, 1)
                if runs(0):
                    n, s = batch(0), slot(0)
                    att_n, rden_n = att[:, s % 2, :, :, :], rden[:, s % 2, :, :]
                    dve.wait_ge(out_in_psum, n * 2 + 2 + START)
                    nc.vector.transpose(att_n.rearrange("p t c g -> p (t c) g"),
                                        out_ps[:, :].rearrange("p (t a c) -> p t c a", t=TT, c=C)).then_inc(att_ready, 1)
                    dve.wait_ge(att_ready, n + 1 + START)
                    nc.vector.reciprocal(rden_n, att_n[:, :, :, G]).then_inc(rden_ready, 1)
                    dve.wait_ge(rden_ready, n + 1)
                    release(dve, final_steps, n * 2 - 3, START)
                    nc.vector.tensor_tensor(
                        normed[:, s % 2, :, :].rearrange("p t (c g) -> p (t c) g", g=G),
                        att_n.rearrange("p t c g -> p (t c) g")[:, :, 0:G],
                        rden_n.rearrange("p t (c a) -> p (t c) a", a=1).to_broadcast([P, TT * C, G]),
                        ALU.mult).then_inc(normed_ready, 1)

            steps(dve, step, before=[(-LEAD_PROJ, first), (-LEAD_PROJ + 1, second), (-LEAD_PROJ + 2, third)])

        @block.tensor
        def _(pe):
            for q in started:
                pe.sem_inc(q, START)

            def biases():
                pe.wait_ge(wqk_ready, 2)
                nc.tensor.matmul(bias_ps[:, 0:1], wq_ord[:, :], beta_col[:, :], start=True, stop=True)
                nc.tensor.matmul(bias_ps[:, 1:2], wk_ord[:, :], beta_col[:, :], start=True, stop=True)\
                  .then_inc(bias_in_psum, 1)
                pe.wait_ge(ident_ready, 2)

            def mixing():
                pe.wait_ge(bias_ready, 1)
                pe.wait_ge(vbias_ready, 1)
                nc.tensor.matmul(vbias_ps, beta_bc[:, :], wv_sum[:, :], start=True, stop=False)
                nc.tensor.matmul(vbias_ps, ones[0:1, :], bv_sum[:, :], start=False, stop=True)
                pe.wait_ge(abias_loaded, 16)
                nc.tensor.matmul(abias_ps, mix_rows[:, :], bsel[:, :], start=True, stop=True)
                pe.wait_ge(mix_ready, 1)
                pe.wait_ge(adapters_loaded, 16 * K)
                for k in range(K):
                    last = nc.tensor.matmul(adapt_ps, wsel[:, k, :], mix_ident[:, k, :], start=(k == 0), stop=(k == K - 1))
                last.then_inc(mixed_in_psum, 1)

            def step(batch, slot, runs):
                def pass1(u):
                    if runs(LEAD_MAX):
                        n, s = batch(LEAD_MAX), slot(LEAD_MAX)
                        if u == 0:
                            pe.wait_ge(stack_loaded[s], stack_count(n, s, LOADS) + START)
                        release(pe, max_done, n * H + u - 1)
                        for t in range(TT):
                            last = nc.tensor.matmul(max_ps[u % 2][:, t, :], stack[0:STACK, s, 0, u, t * P:(t + 1) * P],
                                                    stack[0:STACK, s, 1, u, :], start=True, stop=True)
                        last.then_inc(max_scores, 1)

                def pass2(u):
                    if runs(0):
                        n, s = batch(0), slot(0)
                        if u == 0:
                            pe.wait_ge(rows_loaded[s], (n - s) * (16 // RING) + 16 + START)
                        release(pe, exp_done, n * H + u - 1, START)
                        for t in range(TT):
                            last = nc.tensor.matmul(exp_ps[u % 2][:, t, :], stack[:, s, 1, u, t * P:(t + 1) * P],
                                                    stack[:, s, 0, u, :], start=True, stop=True)
                        last.then_inc(exp_scores, 1)

                def product(group, t):
                    if runs(0):
                        n, s = batch(0), slot(0)
                        if t == 0:
                            pe.wait_ge(exp_done, n * H + (group + 1) * HALF + START)
                        if group == 0 and t == 0:
                            pe.wait_ge(values_ready, n + 1)
                            release(pe, att_ready, n, START)
                        for j in range(HALF):
                            u = group * HALF + j
                            last = nc.tensor.matmul(out_ps[j * A:(j + 1) * A, group * S:(group + 1) * S],
                                                    values[:, s, t, u, :], probs[:, u, t, :],
                                                    start=(t == 0), stop=(t == TT - 1), skip_group_check=True)
                        if t == TT - 1:
                            last.then_inc(out_in_psum, 1)

                def transposes():
                    if runs(LEAD_PROJ):
                        n, s = batch(LEAD_PROJ), slot(LEAD_PROJ)
                        pe.wait_ge(z_ready, n * TT + TT)
                        release(pe, zt_in_sbuf, n)
                        release(pe, nmax_in_sbuf, n - RING + 1)
                        for t in range(TT):
                            last = nc.tensor.transpose(zt_ps[:, t * P:(t + 1) * P], z[:, s, t, :], ident[:, :])
                        last.then_inc(zt_in_psum, 1)

                def maxima():
                    if runs(LEAD_ROWS):
                        n, s = batch(LEAD_ROWS), slot(LEAD_ROWS)
                        pe.wait_ge(nmax_split, n * 2 + 2)
                        if isinstance(n, int):
                            pe.wait_ge(zt_in_sbuf, min(n + LEAD_PROJ - LEAD_ROWS + 1, B))
                        else:
                            pe.wait_ge(zt_in_sbuf, n + (LEAD_PROJ - LEAD_ROWS + 1))
                        nc.tensor.transpose(nmax_ps[0:2 * H * TT, 0:P], nmax_parts[:, s % 2, :], ident_bf[:, :])\
                          .then_inc(nmax_in_psum, 1)

                def queries_keys():
                    if runs(LEAD_PROJ):
                        n, s = batch(LEAD_PROJ), slot(LEAD_PROJ)
                        pe.wait_ge(zt_in_sbuf, n + 1)
                        release(pe, qk_in_sbuf, n * 2)
                        nc.tensor.matmul(qk_ps[:, 0, :], wqg[:, :], zt_sb[:, s, :], start=True, stop=True)
                        nc.tensor.matmul(qk_ps[:, 1, :], wkg[:, :], zt_sb[:, s, :], start=True, stop=True)\
                          .then_inc(qk_in_psum, 1)

                def values_adapters():
                    if runs(LEAD_ROWS):
                        n, s = batch(LEAD_ROWS), slot(LEAD_ROWS)
                        if isinstance(n, int) and n == 0:
                            pe.wait_ge(consts_ready, 1)
                            pe.wait_ge(pool_setup, 3 + RING)
                        release(pe, adapters_ready, n * TT)
                        for t in range(TT):
                            last = nc.tensor.matmul(vy_ps[:, t, :], zt_sb[:, s, t * P:(t + 1) * P], w_vy[:, :],
                                                    start=True, stop=True)
                        last.then_inc(vy_in_psum, 1)

                pass1(0), pass2(0)
                pass1(1), pass2(1)
                transposes()
                pass1(2), pass2(2)
                maxima()
                pass1(3), pass2(3)
                queries_keys()
                pass1(4), pass2(4)
                pass2(5)
                product(0, 0)
                pass1(5), pass2(6)
                product(0, 1)
                pass1(6), pass2(7)
                values_adapters()
                pass1(7)
                product(1, 0)
                product(1, 1)

            steps(pe, step, before=[(-LEAD_PROJ, biases), (-LEAD_PROJ + 2, mixing)])
    return nc


_INS = ['L0_attn_x', 'L0_attn_Wq', 'L0_attn_bq', 'L0_attn_Wk', 'L0_attn_bk', 'L0_attn_Wv', 'L0_attn_bv',
        'L0_attn_gamma', 'L0_attn_beta', 'L0_ffn_W', 'L0_ffn_b', 'L0_ffn_ids', 'L0_ffn_weights']
_OUTS = [((16, 256, 128), 'float32')]


def kernel(**inputs):
    import numpy as _np
    import concourse.bacc as _bacc
    from concourse import mybir as _mybir
    from concourse.bass_utils import run_bass_kernel_spmd as _run

    nc = _bacc.Bacc("TRN2", target_bir_lowering=False, num_devices=1)
    arrays, args = {}, []
    for name in _INS:
        a = _np.ascontiguousarray(inputs[name])
        arrays[f"in_{name}_dram"] = a
        args.append(nc.dram_tensor(f"in_{name}_dram", a.shape, _mybir.dt.from_np(a.dtype), kind="ExternalInput").ap())
    for i, (shape, dtype) in enumerate(_OUTS):
        dt = _mybir.dt.from_np(_np.dtype(dtype))
        args.append(nc.dram_tensor(f"out_{i}_dram", shape, dt, kind="ExternalOutput").ap())
    build(nc, *args)
    r = _run(nc, [arrays], core_ids=[0])
    return r.results[0]["out_0_dram"]
```

```python
from contextlib import ExitStack

import concourse.bass as bass
from concourse import mybir

F32 = mybir.dt.float32
BF16 = mybir.dt.bfloat16
I32 = mybir.dt.int32
ALU = mybir.AluOpType
ACT = mybir.ActivationFunctionType
AX = mybir.AxisListType

P = 128
EPS = 1e-5
RING = 4
LEAD_Z, LEAD_PROJ, LEAD_STACK, LEAD_MAX, LEAD_ROWS, LAG_OUT = 5, 4, 3, 2, 1, -1


def build(nc, x, Wq, bq, Wk, bk, Wv, bv, gamma, beta, W, b, ids, weights, out):
    B, S, D = x.shape
    HG = Wv.shape[1]
    H = HG // D
    DK = D // H
    G = D // H
    K = ids.shape[0]
    N_AD = W.shape[0]
    TT = S // P
    NT = B * TT
    C = D // G
    A = S // C
    STACK = 6 * DK
    ROWS = STACK + 2
    HALF = H // 2
    SCALE = float(DK) ** -0.5
    assert D == P and A == 32 and G * C == D and HALF * A == P and B % RING == 0

    scratch = nc.dram_tensor("parts_dram", (RING, 6, P * S), BF16, kind="Internal").ap()
    x_tiles = x.rearrange("b (t p) d -> p (b t) d", p=P)
    out_tiles = out.rearrange("b (t p) d -> p (b t) d", p=P)

    with ExitStack() as ctx:
        def sb(name, shape, dt=F32):
            return ctx.enter_context(nc.sbuf_tensor(name, shape, dt))

        def ps(name, shape, dt=F32):
            return ctx.enter_context(nc.psum_tensor(name, shape, dt))

        def sem(name):
            return ctx.enter_context(nc.semaphore(name))

        x_flat = sb("x_flat", [P, NT * D])
        x_sb = x_flat[:, :].rearrange("p (n d) -> p n d", d=D)
        wq_sb, wk_sb = sb("wq_sb", [P, D]), sb("wk_sb", [P, D])
        wq_ord, wk_ord = sb("wq_ord", [P, D]), sb("wk_ord", [P, D])
        wqg, wkg = sb("wqg", [P, D]), sb("wkg", [P, D])
        wv_sb = sb("wv_sb", [P, HG])
        bv_sb = sb("bv_sb", [H * G, H])
        wsel = sb("wsel", [P, K, D])
        bsel = sb("bsel", [K, D])
        ids_sb, ids_col = sb("ids_sb", [1, K], I32), sb("ids_col", [K, 1], I32)
        mix_all = sb("mix_all", [P, K])
        mix_col = sb("mix_col", [K, 1])
        mix_rows = sb("mix_rows", [K, P])
        gamma_col, beta_col = sb("gamma_col", [P, 1]), sb("beta_col", [P, 1])
        bq_col, bk_col = sb("bq_col", [P, 1]), sb("bk_col", [P, 1])
        bias_qk = sb("bias_qk", [P, 2])
        ones = sb("ones", [P, P])
        warm = sb("warm", [P, 2])
        zeros = sb("zeros", [P, 2 * S])
        ident = sb("ident", [P, P])
        ident_bf = sb("ident_bf", [P, P], BF16)
        mix_ident = sb("mix_ident", [P, K, P])
        beta_bc = sb("beta_bc", [P, P])
        wv_sum = sb("wv_sum", [P, H * G])
        bv_sum, bv_diag = sb("bv_sum", [H * G, 1]), sb("bv_diag", [H * G, P])
        wv_four, wv_two = sb("wv_four", [P, H * G, H // 2]), sb("wv_two", [P, H * G, H // 4])
        w_vy = sb("w_vy", [P, 2 * D])
        adapter_bias = sb("adapter_bias", [P, D])
        out_bias = sb("out_bias", [P, TT, D])
        bn = sb("bn", [P, NT, 6])
        mean_var = sb("mean_var", [P, NT * 2])
        var_in, std0, rstd0 = sb("var_in", [P, 2, NT]), sb("std0", [P, 2, NT]), sb("rstd0", [P, 2, NT])
        std, rstd = sb("std", [P, 2, NT]), sb("rstd", [P, 2, NT])
        rstd_flat = rstd[:, :, :].rearrange("p a n -> p (a n)")
        ratio = sb("ratio", [P, NT])
        z = sb("z", [P, RING, TT, D])
        zt_sb = sb("zt_sb", [P, RING, S])
        qk32 = sb("qk32", [P, 2, 2, S])
        rest = sb("rest", [P, 2, S])
        parts = sb("parts", [P, 2, 6, S], BF16)
        stack = sb("stack", [ROWS, RING, 2, H, S], BF16)
        nmax = sb("nmax", [P, 2, H * TT])
        nmax_parts = sb("nmax_parts", [P, 2, 2 * H * TT], BF16)
        nmax_rows = sb("nmax_rows", [2 * H * TT, 2, P], BF16)
        probs = sb("probs", [P, H, TT, S])
        values = sb("values", [P, RING, TT, H, 2 * G])
        adapters = sb("adapters", [P, RING, TT, D])
        att = sb("att", [P, 2, TT, C, 2 * G])
        rden = sb("rden", [P, 2, TT, C])
        normed = sb("normed", [P, 2, TT, D])
        summed = sb("summed", [P, 2, TT, D])
        result = sb("result", [P, 2, TT, D])

        max_ps = [ps(f"max_ps{i}", [P, TT, S]) for i in range(2)]
        exp_ps = [ps(f"exp_ps{i}", [P, TT, S]) for i in range(2)]
        out_ps = ps("out_ps", [P, 2 * S])
        zt_ps = ps("zt_ps", [P, 2 * S])
        qk_ps = ps("qk_ps", [P, 2, S])
        vy_ps = ps("vy_ps", [P, TT, 2 * D])
        nmax_ps = zt_ps[:, S:2 * S].bitcast(BF16)
        bias_ps = exp_ps[0][:, 0, 0:2]
        vbias_ps = exp_ps[0][:, 0, P:2 * P]
        abias_ps = exp_ps[0][:, 1, 0:P]
        adapt_ps = exp_ps[1][:, 0, 0:P]

        x_first, x_second, x_third = sem("x_first"), sem("x_second"), sem("x_third")
        ids_loaded, qk_loaded, wv_loaded = sem("ids_loaded"), sem("qk_loaded"), sem("wv_loaded")
        bias_loaded, bv_loaded = sem("bias_loaded"), sem("bv_loaded")
        mix_loaded, adapters_loaded, abias_loaded = sem("mix_loaded"), sem("adapters_loaded"), sem("abias_loaded")
        ones_ready, ident_ready, pool_setup, dve_setup = sem("ones_ready"), sem("ident_ready"), sem("pool_setup"), sem("dve_setup")
        var_ready, std_ready, wqk_ready, bias_ready = sem("var_ready"), sem("std_ready"), sem("wqk_ready"), sem("bias_ready")
        wv_summed = sem("wv_summed")
        bias_in_psum, vbias_ready, mix_ready = sem("bias_in_psum"), sem("vbias_ready"), sem("mix_ready")
        mixed_in_psum, consts_ready = sem("mixed_in_psum"), sem("consts_ready")
        z_ready, zt_in_psum, zt_in_sbuf = sem("z_ready"), sem("zt_in_psum"), sem("zt_in_sbuf")
        qk_in_psum, qk_in_sbuf = sem("qk_in_psum"), sem("qk_in_sbuf")
        split_steps, parts_stored = sem("split_steps"), sem("parts_stored")
        stack_loaded = [sem(f"stack_loaded{i}") for i in range(RING)]
        rows_loaded = [sem(f"rows_loaded{i}") for i in range(RING)]
        max_scores, max_done, nmax_split = sem("max_scores"), sem("max_done"), sem("nmax_split")
        nmax_in_psum, nmax_in_sbuf = sem("nmax_in_psum"), sem("nmax_in_sbuf")
        exp_scores, exp_done, out_in_psum = sem("exp_scores"), sem("exp_done"), sem("out_in_psum")
        vy_in_psum, values_ready, adapters_ready = sem("vy_in_psum"), sem("values_ready"), sem("adapters_ready")
        att_ready, rden_ready, normed_ready = sem("att_ready"), sem("rden_ready"), sem("normed_ready")
        final_steps = sem("final_steps")
        stored = [sem(f"stored{i}") for i in range(2)]

        def steps(engine, step, before=()):
            def one(t, base):
                step(lambda lead: base + (t + lead), lambda lead: (t + lead) % RING,
                     lambda lead: not isinstance(base, int) or 0 <= t + lead < B)

            first = -LAG_OUT
            turns = (B - LEAD_Z - first) // RING
            for t in range(-LEAD_Z, first):
                for work in [w for at, w in before if at == t]:
                    work()
                one(t, 0)
            with engine.Fori(0, turns) as i:
                for t in range(first, first + RING):
                    one(t, i * RING)
            for t in range(first + turns * RING, B - LAG_OUT):
                one(t, 0)

        START = 16
        started = [out_in_psum, final_steps, exp_scores, exp_done, att_ready, *stack_loaded, *rows_loaded, *stored]

        def release(engine, semaphore, value, start=0):
            if not isinstance(value, int) or value > 0:
                engine.wait_ge(semaphore, value + start)

        STATS = [(0, TT), (TT, 4 * TT), (4 * TT, NT)]
        LOADS = 3

        def stack_count(n, s, more):
            return (n - s) * (LOADS * 16 // RING) + more * 16

        block = ctx.enter_context(nc.Block())

        @block.sync
        def _(sp):
            sp.dma_start(x_sb[:, 0:TT, :], x_tiles[:, 0:TT, :]).then_inc(x_first, 16)
            sp.dma_start(wq_sb[:, :], Wq).then_inc(qk_loaded, 16)
            sp.dma_start(gamma_col[:, :], gamma.rearrange("(p a) -> p a", a=1)).then_inc(qk_loaded, 16)
            sp.dma_start(wk_sb[:, :], Wk).then_inc(qk_loaded, 16)
            sp.dma_start(beta_col[:, :], beta.rearrange("(p a) -> p a", a=1)).then_inc(bias_loaded, 16)
            with nc.allow_non_contiguous_dma(reason="two vectors of 128 numbers, reordered"):
                for bias, col in ((bq, bq_col), (bk, bk_col)):
                    sp.dma_start(col[:, :], bias.rearrange("(h k a) -> k h a", k=DK, a=1)).then_inc(bias_loaded, 16)
            sp.dma_start(x_sb[:, TT:4 * TT, :], x_tiles[:, TT:4 * TT, :]).then_inc(x_second, 16)
            sp.dma_start(ids_sb[:, :], ids.rearrange("(a k) -> a k", a=1)).then_inc(ids_loaded, 16)
            sp.dma_start(ids_col[:, :], ids.rearrange("(k a) -> k a", a=1)).then_inc(ids_loaded, 16)
            sp.dma_start(wv_sb[:, :], Wv).then_inc(wv_loaded, 16)
            sp.dma_start(bv_sb[:, :], bv.rearrange("(n j) -> n j", j=H)).then_inc(bv_loaded, 16)
            sp.dma_start(x_sb[:, 4 * TT:NT, :], x_tiles[:, 4 * TT:NT, :]).then_inc(x_third, 16)
            sp.dma_start(mix_all[:, :], weights.rearrange("(a k) -> a k", a=1).to_broadcast([P, K]))\
              .then_inc(mix_loaded, 16)
            sp.dma_start(mix_col[:, :], weights.rearrange("(k a) -> k a", a=1)).then_inc(mix_loaded, 16)

            sp.wait_ge(ids_loaded, 32)
            for k in range(K):
                which = sp.value_load(ids_sb[0:1, k:k + 1], min_val=0, max_val=N_AD - 1)
                sp.dma_start(wsel[:, k, :], W[bass.ds(which, 1)].rearrange("n o i -> o (n i)"))\
                  .then_inc(adapters_loaded, 16)

            def step(batch, slot, runs):
                if runs(LEAD_STACK):
                    n, s = batch(LEAD_STACK), slot(LEAD_STACK)
                    release(sp, exp_scores, (n - RING + 1) * H, START)
                    sp.wait_ge(parts_stored, n * 16 + 16)
                    row = 0
                    for count in (3, 2, 1):
                        sp.dma_start(
                            stack[row:row + count * DK, s, :, :, :].rearrange("r a h s -> r a (h s)"),
                            scratch[s, 3 - count:3 + count, :].rearrange("(a r) (k n) -> (r k) a n", a=2, k=DK))\
                          .then_inc(stack_loaded[s], 16)
                        row += count * DK
                if runs(LEAD_ROWS):
                    n, s = batch(LEAD_ROWS), slot(LEAD_ROWS)
                    sp.wait_ge(nmax_in_sbuf, n + 1)
                    sp.dma_start(stack[STACK:ROWS, s, 0, :, :].rearrange("r h s -> r (h s)"),
                                 nmax_rows[:, s % 2, :]).then_inc(rows_loaded[s], 16)
                if runs(LEAD_PROJ):
                    n, s = batch(LEAD_PROJ), slot(LEAD_PROJ)
                    release(sp, stack_loaded[s], stack_count(n, s, 0), START)
                    sp.wait_ge(split_steps, n * 3 + 3)
                    sp.dma_start(scratch[s].rearrange("r (p s) -> p r s", p=P), parts[:, s % 2, :, :])\
                      .then_inc(parts_stored, 16)
                if runs(LAG_OUT):
                    n, s = batch(LAG_OUT), slot(LAG_OUT)
                    sp.wait_ge(final_steps, n * 2 + 2 + START)
                    sp.dma_start(out_tiles[:, bass.ds(n * TT, TT), :], result[:, s % 2, :, :])\
                      .then_inc(stored[s % 2], 16)

            steps(sp, step)
            for q in stored:
                sp.wait_ge(q, 16 * B // 2 + START)

        @block.gpsimd
        def _(pool):
            pool.memset(ident[:, :], 0.0).then_inc(pool_setup, 1)
            pool.memset(zeros[:, :], 0.0).then_inc(pool_setup, 1)
            pool.wait_ge(pool_setup, 2)
            pool.affine_select(out=ident[:, :], in_=ident[:, :], compare_op=ALU.not_equal, fill=1.0, base=0,
                               pattern=[[-1, P]], channel_multiplier=1).then_inc(ident_ready, 1)
            pool.wait_ge(ident_ready, 1)
            pool.tensor_tensor(ident_bf[:, :], ident[:, :], zeros[:, 0:P], ALU.add).then_inc(ident_ready, 1)

            pool.wait_ge(ident_ready, 2)
            pool.memset(stack[STACK:ROWS, 0, 1, :, :], 1.0).then_inc(pool_setup, 1)
            pool.wait_ge(pool_setup, 3)
            pool.wait_ge(ids_loaded, 32)
            pool.indirect_dma_start(bsel[:, :], None, b, bass.IndirectOffsetOnAxis(ap=ids_col[:, 0:1], axis=0))\
                .then_inc(abias_loaded, 16)

            pool.wait_ge(wv_loaded, 16)
            summand = wv_sb[:, :].rearrange("p (n j) -> p n j", j=H)
            for done, total in enumerate((wv_four[:, :, :], wv_two[:, :, :],
                                          wv_sum[:, :].rearrange("p (n a) -> p n a", a=1))):
                half = total.shape[2]
                if done:
                    pool.wait_ge(wv_summed, done)
                pool.tensor_tensor(total, summand[:, :, 0:half], summand[:, :, half:2 * half], ALU.add)\
                    .then_inc(wv_summed, 1)
                summand = total

            def constants():
                pool.memset(values[:, :, :, :, G:2 * G], 1.0).then_inc(pool_setup, 1)
                for s in range(1, RING):
                    pool.wait_ge(pool_setup, 3 + s)
                    pool.memset(stack[STACK:ROWS, s, 1, :, :], 1.0).then_inc(pool_setup, 1)
                pool.wait_ge(pool_setup, 3 + RING)

            def step(batch, slot, runs):
                if runs(LEAD_ROWS):
                    n, s = batch(LEAD_ROWS), slot(LEAD_ROWS)
                    nmax_n = nmax[:, s % 2, :]
                    high, low = nmax_parts[:, s % 2, 0:H * TT], nmax_parts[:, s % 2, H * TT:2 * H * TT]
                    pool.wait_ge(max_done, n * H + H)
                    release(pool, nmax_in_psum, n - 1)
                    pool.tensor_tensor(high, nmax_n, zeros[:, 0:H * TT], ALU.add).then_inc(nmax_split, 1)
                    pool.wait_ge(nmax_split, n * 2 + 1)
                    pool.tensor_tensor(low, nmax_n, high, ALU.subtract).then_inc(nmax_split, 1)
                if runs(LEAD_PROJ):
                    n, s = batch(LEAD_PROJ), slot(LEAD_PROJ)
                    qk_n, none = qk32[:, s % 2, :, :], zeros[:, :].rearrange("p (a s) -> p a s", a=2)
                    low, middle, high = parts[:, s % 2, 0:6:5, :], parts[:, s % 2, 1:5:3, :], parts[:, s % 2, 2:4, :]
                    pool.wait_ge(qk_in_sbuf, n * 2 + 2)
                    release(pool, split_steps, n * 3)
                    pool.tensor_tensor(rest[:, :, :], qk_n, high, ALU.subtract).then_inc(split_steps, 1)
                    pool.wait_ge(split_steps, n * 3 + 1)
                    pool.tensor_tensor(middle, rest[:, :, :], none, ALU.add).then_inc(split_steps, 1)
                    pool.wait_ge(split_steps, n * 3 + 2)
                    pool.tensor_tensor(low, rest[:, :, :], middle, ALU.subtract).then_inc(split_steps, 1)
                if runs(LAG_OUT):
                    n, s = batch(LAG_OUT), slot(LAG_OUT)
                    summed_n = summed[:, s % 2, :, :].rearrange("p t d -> p (t d)")
                    pool.wait_ge(adapters_ready, n * TT + TT)
                    pool.wait_ge(normed_ready, n + 1)
                    pool.tensor_tensor(summed_n, normed[:, s % 2, :, :].rearrange("p t d -> p (t d)"),
                                       adapters[:, s, :, :].rearrange("p t d -> p (t d)"), ALU.add)\
                        .then_inc(final_steps, 1)
                    pool.wait_ge(final_steps, n * 2 + 1 + START)
                    release(pool, stored[s % 2], (n - s % 2) * 8, START)
                    pool.tensor_tensor(result[:, s % 2, :, :].rearrange("p t d -> p (t d)"), summed_n,
                                       x_flat[:, bass.ds(n * TT * D, TT * D)], ALU.add).then_inc(final_steps, 1)

            steps(pool, step, before=[(-LEAD_PROJ + 2, constants)])

        @block.scalar
        def _(act):
            act.wait_ge(ones_ready, 1)
            nc.scalar.activation(warm[:, 0:1], ones[:, 0:1], ACT.Sqrt)

            def roots(group):
                def work():
                    lo, hi = STATS[group]
                    act.wait_ge(var_ready, 2 * group + 2)
                    nc.scalar.activation(std0[:, :, lo:hi], var_in[:, :, lo:hi], ACT.Sqrt).then_inc(std_ready, 1)
                    if hi == NT:
                        nc.scalar.activation(warm[:, 1:2], ones[:, 0:1], ACT.Exp)
                return work

            def diagonals():
                act.wait_ge(mix_loaded, 32)
                act.wait_ge(ident_ready, 1)
                for k in range(K):
                    last = nc.scalar.activation(mix_ident[:, k, :], ident[:, :], ACT.Copy, scale=mix_all[:, k:k + 1])
                last.then_inc(mix_ready, 1)

            def step(batch, slot, runs):
                def exponentials(*heads):
                    for u in heads if runs(0) else ():
                        n = batch(0)
                        act.wait_ge(exp_scores, n * H + u + 1 + START)
                        if u % HALF == 0:
                            release(act, out_in_psum, n * 2 + (u // HALF - 1), START)
                        nc.scalar.activation(probs[:, u, :, :], exp_ps[u % 2][:, :, :], ACT.Exp, scale=SCALE)\
                          .then_inc(exp_done, 1)

                def tokens():
                    if runs(LEAD_Z):
                        n, s = batch(LEAD_Z), slot(LEAD_Z)
                        act.wait_ge(zt_in_psum, n + 1)
                        release(act, vy_in_psum, n - RING + 1)
                        nc.scalar.activation(zt_sb[:, s, :], zt_ps[:, 0:S], ACT.Copy).then_inc(zt_in_sbuf, 1)

                def queries_keys():
                    if runs(LEAD_PROJ):
                        n, s = batch(LEAD_PROJ), slot(LEAD_PROJ)
                        act.wait_ge(qk_in_psum, n + 1)
                        release(act, split_steps, (n - 2) * 3 + 1)
                        release(act, parts_stored, (n - 1) * 16)
                        if isinstance(n, int) and n == 0:
                            act.wait_ge(bias_ready, 1)
                        for side in range(2):
                            bias = bias_qk[:, side:side + 1]
                            nc.scalar.activation(qk32[:, s % 2, side, :], qk_ps[:, side, :], ACT.Identity, bias=bias)
                            nc.scalar.activation(parts[:, s % 2, 2 + side, :], qk_ps[:, side, :], ACT.Identity,
                                                 bias=bias).then_inc(qk_in_sbuf, 1)

                def maxima():
                    if runs(LEAD_ROWS):
                        n, s = batch(LEAD_ROWS), slot(LEAD_ROWS)
                        act.wait_ge(nmax_in_psum, n + 1)
                        if not isinstance(n, int) or n >= 2:
                            before = (s - 2) % RING
                            act.wait_ge(rows_loaded[before],
                                        n * (16 // RING) + (16 - (2 + before) * (16 // RING) + START))
                        nc.scalar.activation(nmax_rows[:, s % 2, :], nmax_ps[0:2 * H * TT, 0:P], ACT.Copy)\
                          .then_inc(nmax_in_sbuf, 1)

                def value_columns():
                    if runs(LEAD_ROWS):
                        n, s = batch(LEAD_ROWS), slot(LEAD_ROWS)
                        act.wait_ge(vy_in_psum, n + 1)
                        release(act, out_in_psum, n * 2 - 2 * (RING - 1), START)
                        for t in range(TT):
                            last = nc.scalar.activation(values[:, s, t, :, 0:G],
                                                        vy_ps[:, t, 0:D].rearrange("p (h g) -> p h g", g=G), ACT.Copy)
                        last.then_inc(values_ready, 1)

                queries_keys()
                exponentials(0, 1, 2)
                maxima()
                exponentials(3)
                value_columns()
                exponentials(4, 5)
                tokens()
                exponentials(6, 7)

            steps(act, step, before=[(-LEAD_Z, roots(0)), (-LEAD_Z + 1, roots(1)), (-LEAD_STACK, diagonals), (-LEAD_ROWS, roots(2))])

        @block.vector
        def _(dve):
            done = [0]

            def link(ins):
                done[0] += 1
                ins.then_inc(dve_setup, 1)
                dve.wait_ge(dve_setup, done[0])

            mv = mean_var[:, :].rearrange("p (n a) -> p n a", a=2)

            def statistics(group):
                lo, hi = STATS[group]
                dve.wait_ge((x_first, x_second, x_third)[group], 16)
                for n in range(lo, hi):
                    last = nc.vector.bn_stats(bn[:, n, :], x_sb[:, n, :])
                link(last)
                for n in range(lo, hi):
                    last = nc.vector.bn_aggr(mv[:, n, :], bn[:, n, :])
                link(last)
                nc.vector.tensor_scalar(var_in[:, 0, lo:hi], mv[:, lo:hi, 1], EPS, None, ALU.add).then_inc(var_ready, 1)
                nc.vector.tensor_scalar(var_in[:, 1, lo:hi], mv[:, lo:hi, 1], 1.0 + EPS, EPS * EPS,
                                        ALU.mult, ALU.add).then_inc(var_ready, 1)

            def deviations(group):
                lo, hi = STATS[group]
                v, s0, r0 = var_in[:, :, lo:hi], std0[:, :, lo:hi], rstd0[:, :, lo:hi]
                s1, r1 = std[:, :, lo:hi], rstd[:, :, lo:hi]
                dve.wait_ge(std_ready, group + 1)
                link(nc.vector.reciprocal(r0, s0))
                link(nc.vector.tensor_tensor(s1, v, r0, ALU.mult))
                link(nc.vector.tensor_tensor(s1, s1, s0, ALU.add))
                link(nc.vector.tensor_scalar(s1, s1, 0.5, None, ALU.mult))
                link(nc.vector.reciprocal(r1, s1))
                link(nc.vector.tensor_tensor(ratio[:, lo:hi], std[:, 1, lo:hi], rstd[:, 0, lo:hi], ALU.mult))

            def first():
                nc.vector.memset(ones[:, :], 1.0).then_inc(ones_ready, 1)
                statistics(0)
                deviations(0)

            def second():
                dve.wait_ge(qk_loaded, 48)
                for w, ordered, scaled in ((wq_sb, wq_ord, wqg), (wk_sb, wk_ord, wkg)):
                    by_column = w[:, :].rearrange("p (h k) -> p k h", k=DK)
                    nc.vector.tensor_copy(ordered[:, :].rearrange("p (k h) -> p k h", k=DK), by_column)
                    nc.vector.tensor_scalar(scaled[:, :].rearrange("p (k h) -> p k h", k=DK), by_column,
                                            gamma_col[:, :], None, ALU.mult).then_inc(wqk_ready, 1)
                dve.wait_ge(bias_in_psum, 1)
                dve.wait_ge(bias_loaded, 48)
                nc.vector.tensor_tensor(bias_qk[:, 0:1], bias_ps[:, 0:1], bq_col[:, :], ALU.add)
                nc.vector.tensor_tensor(bias_qk[:, 1:2], bias_ps[:, 1:2], bk_col[:, :], ALU.add).then_inc(bias_ready, 1)
                statistics(1)
                deviations(1)

            def third():
                dve.wait_ge(bv_loaded, 16)
                link(nc.vector.tensor_reduce(bv_sum[:, :], bv_sb[:, :], AX.X, ALU.add))
                dve.wait_ge(ident_ready, 1)
                nc.vector.tensor_scalar(bv_diag[:, :], ident[:, :], bv_sum[:, :], None, ALU.mult)
                nc.vector.tensor_scalar(beta_bc[:, :], ones[:, :], beta_col[:, :], None, ALU.mult)
                dve.wait_ge(mix_loaded, 32)
                nc.vector.tensor_scalar(mix_rows[:, :], ones[0:K, :], mix_col[:, :], None, ALU.mult).then_inc(vbias_ready, 1)
                dve.wait_ge(wv_summed, 3)
                nc.vector.tensor_scalar(w_vy[:, 0:D], wv_sum[:, :], gamma_col[:, :], None, ALU.mult)
                statistics(2)
                dve.wait_ge(mixed_in_psum, 1)
                nc.vector.tensor_copy(w_vy[:, D:2 * D], adapt_ps)
                link(nc.vector.tensor_copy(adapter_bias[:, :], abias_ps))
                for t in range(TT):
                    for j in range(HALF):
                        q = slice(A * j, A * j + A)
                        head = (t * HALF + j) * G
                        last = nc.vector.tensor_tensor(
                            out_bias[q, t, :].rearrange("p (c g) -> p c g", g=G),
                            vbias_ps[q, head:head + G].rearrange("p (a g) -> p a g", a=1).to_broadcast([A, C, G]),
                            adapter_bias[q, :].rearrange("p (c g) -> p c g", g=G), ALU.add)
                last.then_inc(consts_ready, 1)

            def fourth():
                deviations(2)

            def step(batch, slot, runs):
                def maxima(*heads):
                    n, s = batch(LEAD_MAX), slot(LEAD_MAX)
                    for u in heads if runs(LEAD_MAX) else ():
                        if u == 0:
                            release(dve, nmax_split, (n - 1) * 2)
                        dve.wait_ge(max_scores, n * H + u + 1)
                        nc.vector.tensor_reduce(nmax[:, s % 2, u * TT:(u + 1) * TT], max_ps[u % 2][:, :, :], AX.X,
                                                ALU.max, negate=True).then_inc(max_done, 1)

                def mixture(t):
                    n, s = batch(LEAD_ROWS), slot(LEAD_ROWS)
                    if runs(LEAD_ROWS):
                        if t == 0:
                            dve.wait_ge(values_ready, n + 1)
                            release(dve, final_steps, n * 2 - 2 * (RING - 1), START)
                        nc.vector.scalar_tensor_tensor(adapters[:, s, t, :], vy_ps[:, t, D:2 * D],
                                                       ratio[:, bass.ds(n * TT + t, 1)], out_bias[:, t, :],
                                                       ALU.mult, ALU.add).then_inc(adapters_ready, 1)

                def normalized():
                    n, s = batch(LEAD_Z), slot(LEAD_Z)
                    if runs(LEAD_Z):
                        release(dve, zt_in_psum, n - RING + 1)
                    for t in range(TT) if runs(LEAD_Z) else ():
                        tile = n * TT + t
                        nc.vector.tensor_scalar(z[:, s, t, :], x_flat[:, bass.ds(tile * D, D)],
                                                mean_var[:, bass.ds(tile * 2, 1)], rstd_flat[:, bass.ds(tile + NT, 1)],
                                                ALU.subtract, ALU.mult).then_inc(z_ready, 1)

                o, s = batch(LAG_OUT), slot(LAG_OUT)
                att_o, rden_o = att[:, s % 2, :, :, :], rden[:, s % 2, :, :]
                maxima(0, 1)
                normalized()
                maxima(2)
                if runs(LAG_OUT):
                    dve.wait_ge(out_in_psum, o * 2 + 2 + START)
                    nc.vector.transpose(att_o.rearrange("p t c g -> p (t c) g"),
                                        out_ps[:, :].rearrange("p (t a c) -> p t c a", t=TT, c=C)).then_inc(att_ready, 1)
                maxima(3)
                if runs(LAG_OUT):
                    dve.wait_ge(att_ready, o + 1 + START)
                    nc.vector.reciprocal(rden_o, att_o[:, :, :, G]).then_inc(rden_ready, 1)
                maxima(4)
                if runs(LAG_OUT):
                    dve.wait_ge(rden_ready, o + 1)
                    release(dve, final_steps, o * 2 - 3, START)
                    nc.vector.tensor_tensor(
                        normed[:, s % 2, :, :].rearrange("p t (c g) -> p (t c) g", g=G),
                        att_o.rearrange("p t c g -> p (t c) g")[:, :, 0:G],
                        rden_o.rearrange("p t (c a) -> p (t c) a", a=1).to_broadcast([P, TT * C, G]),
                        ALU.mult).then_inc(normed_ready, 1)
                maxima(5)
                mixture(0)
                mixture(1)
                maxima(6, 7)

            steps(dve, step, before=[(-LEAD_Z, first), (-LEAD_Z + 1, second), (-LEAD_MAX, third), (-LEAD_ROWS, fourth)])

        @block.tensor
        def _(pe):
            for q in started:
                pe.sem_inc(q, START)
            pe.wait_ge(ident_ready, 2)

            def biases():
                pe.wait_ge(wqk_ready, 2)
                pe.wait_ge(bias_loaded, 48)
                nc.tensor.matmul(bias_ps[:, 0:1], wq_ord[:, :], beta_col[:, :], start=True, stop=True)
                nc.tensor.matmul(bias_ps[:, 1:2], wk_ord[:, :], beta_col[:, :], start=True, stop=True)\
                  .then_inc(bias_in_psum, 1)

            def mixing():
                pe.wait_ge(bias_ready, 1)
                pe.wait_ge(vbias_ready, 1)
                pe.wait_ge(wv_summed, 3)
                nc.tensor.matmul(vbias_ps, beta_bc[:, :], wv_sum[:, :], start=True, stop=False)
                nc.tensor.matmul(vbias_ps, ones[:, :], bv_diag[:, :], start=False, stop=True)
                pe.wait_ge(abias_loaded, 16)
                nc.tensor.matmul(abias_ps, mix_rows[:, :], bsel[:, :], start=True, stop=True)
                pe.wait_ge(mix_ready, 1)
                pe.wait_ge(adapters_loaded, 16 * K)
                for k in range(K):
                    last = nc.tensor.matmul(adapt_ps, wsel[:, k, :], mix_ident[:, k, :], start=(k == 0), stop=(k == K - 1))
                last.then_inc(mixed_in_psum, 1)

            def step(batch, slot, runs):
                def pass1(u):
                    if runs(LEAD_MAX):
                        n, s = batch(LEAD_MAX), slot(LEAD_MAX)
                        if u == 0:
                            pe.wait_ge(stack_loaded[s], stack_count(n, s, LOADS) + START)
                        release(pe, max_done, n * H + u - 1)
                        for t in range(TT):
                            last = nc.tensor.matmul(max_ps[u % 2][:, t, :], stack[0:STACK, s, 0, u, t * P:(t + 1) * P],
                                                    stack[0:STACK, s, 1, u, :], start=True, stop=True)
                        last.then_inc(max_scores, 1)

                def pass2(u):
                    if runs(0):
                        n, s = batch(0), slot(0)
                        if u == 0:
                            pe.wait_ge(rows_loaded[s], (n - s) * (16 // RING) + 16 + START)
                        release(pe, exp_done, n * H + u - 1, START)
                        for t in range(TT):
                            last = nc.tensor.matmul(exp_ps[u % 2][:, t, :], stack[:, s, 1, u, t * P:(t + 1) * P],
                                                    stack[:, s, 0, u, :], start=True, stop=True)
                        last.then_inc(exp_scores, 1)

                def product(lead, group, t):
                    if runs(lead):
                        n, s = batch(lead), slot(lead)
                        if t == 0:
                            pe.wait_ge(exp_done, n * H + (group + 1) * HALF + START)
                        if group == 0 and t == 0:
                            pe.wait_ge(values_ready, n + 1)
                            release(pe, att_ready, n, START)
                        for j in range(HALF):
                            u = group * HALF + j
                            last = nc.tensor.matmul(out_ps[j * A:(j + 1) * A, group * S:(group + 1) * S],
                                                    values[:, s, t, u, :], probs[:, u, t, :],
                                                    start=(t == 0), stop=(t == TT - 1), skip_group_check=True)
                        if t == TT - 1:
                            last.then_inc(out_in_psum, 1)

                def transposes():
                    if runs(LEAD_Z):
                        n, s = batch(LEAD_Z), slot(LEAD_Z)
                        pe.wait_ge(z_ready, n * TT + TT)
                        release(pe, zt_in_sbuf, n)
                        release(pe, nmax_in_sbuf, n - RING + 1)
                        for t in range(TT):
                            last = nc.tensor.transpose(zt_ps[:, t * P:(t + 1) * P], z[:, s, t, :], ident[:, :])
                        last.then_inc(zt_in_psum, 1)

                def maxima():
                    if runs(LEAD_ROWS):
                        n, s = batch(LEAD_ROWS), slot(LEAD_ROWS)
                        pe.wait_ge(nmax_split, n * 2 + 2)
                        if isinstance(n, int):
                            pe.wait_ge(zt_in_sbuf, min(n + LEAD_PROJ - LEAD_ROWS + 1, B))
                        else:
                            pe.wait_ge(zt_in_sbuf, n + (LEAD_PROJ - LEAD_ROWS + 1))
                        nc.tensor.transpose(nmax_ps[0:2 * H * TT, 0:P], nmax_parts[:, s % 2, :], ident_bf[:, :])\
                          .then_inc(nmax_in_psum, 1)

                def queries_keys():
                    if runs(LEAD_PROJ):
                        n, s = batch(LEAD_PROJ), slot(LEAD_PROJ)
                        pe.wait_ge(zt_in_sbuf, n + 1)
                        release(pe, qk_in_sbuf, n * 2)
                        for side, w in enumerate((wqg, wkg)):
                            last = nc.tensor.matmul(qk_ps[:, side, :], w[:, :], zt_sb[:, s, :], start=True, stop=True)
                        last.then_inc(qk_in_psum, 1)

                def values_adapters():
                    if runs(LEAD_ROWS):
                        n, s = batch(LEAD_ROWS), slot(LEAD_ROWS)
                        if isinstance(n, int) and n == 0:
                            pe.wait_ge(consts_ready, 1)
                            pe.wait_ge(pool_setup, 3 + RING)
                        release(pe, adapters_ready, n * TT)
                        for t in range(TT):
                            last = nc.tensor.matmul(vy_ps[:, t, :], zt_sb[:, s, t * P:(t + 1) * P], w_vy[:, :],
                                                    start=True, stop=True)
                        last.then_inc(vy_in_psum, 1)

                filling = not runs(0)
                if filling:
                    queries_keys()
                pass1(0)
                if not filling:
                    queries_keys()
                pass1(1), pass2(0)
                product(LAG_OUT, 1, 0)
                pass1(2), pass2(1)
                product(LAG_OUT, 1, 1)
                pass1(3), pass2(2)
                maxima()
                pass1(4), pass2(3)
                values_adapters()
                pass1(5), pass2(4)
                pass1(6), pass2(5)
                product(0, 0, 0)
                transposes()
                pass1(7), pass2(6)
                product(0, 0, 1)
                pass2(7)

            steps(pe, step, before=[(-LEAD_PROJ, biases), (-LEAD_MAX, mixing)])
    return nc


_INS = ['L0_attn_x', 'L0_attn_Wq', 'L0_attn_bq', 'L0_attn_Wk', 'L0_attn_bk', 'L0_attn_Wv', 'L0_attn_bv',
        'L0_attn_gamma', 'L0_attn_beta', 'L0_ffn_W', 'L0_ffn_b', 'L0_ffn_ids', 'L0_ffn_weights']
_OUTS = [((16, 256, 128), 'float32')]


def kernel(**inputs):
    import numpy as _np
    import concourse.bacc as _bacc
    from concourse import mybir as _mybir
    from concourse.bass_utils import run_bass_kernel_spmd as _run

    nc = _bacc.Bacc("TRN2", target_bir_lowering=False, num_devices=1)
    arrays, args = {}, []
    for name in _INS:
        a = _np.ascontiguousarray(inputs[name])
        arrays[f"in_{name}_dram"] = a
        args.append(nc.dram_tensor(f"in_{name}_dram", a.shape, _mybir.dt.from_np(a.dtype), kind="ExternalInput").ap())
    for i, (shape, dtype) in enumerate(_OUTS):
        dt = _mybir.dt.from_np(_np.dtype(dtype))
        args.append(nc.dram_tensor(f"out_{i}_dram", shape, dt, kind="ExternalOutput").ap())
    build(nc, *args)
    r = _run(nc, [arrays], core_ids=[0])
    return r.results[0]["out_0_dram"]
```

```python
from contextlib import ExitStack

import concourse.bass as bass
from concourse import mybir

F32 = mybir.dt.float32
BF16 = mybir.dt.bfloat16
I32 = mybir.dt.int32
ALU = mybir.AluOpType
ACT = mybir.ActivationFunctionType
AX = mybir.AxisListType

P = 128
EPS = 1e-5
RING = 4
LEAD_Z, LEAD_PROJ, LEAD_STACK, LEAD_MAX, LEAD_ROWS, LAG_OUT = 5, 4, 3, 2, 1, -1


def build(nc, x, Wq, bq, Wk, bk, Wv, bv, gamma, beta, W, b, ids, weights, out):
    B, S, D = x.shape
    HG = Wv.shape[1]
    H = HG // D
    DK = D // H
    G = D // H
    K = ids.shape[0]
    N_AD = W.shape[0]
    TT = S // P
    NT = B * TT
    C = D // G
    A = S // C
    STACK = 6 * DK
    ROWS = STACK + 2
    HALF = H // 2
    SCALE = float(DK) ** -0.5
    assert D == P and A == 32 and G * C == D and HALF * A == P and B % RING == 0

    scratch = nc.dram_tensor("parts_dram", (RING, 6, P * S), BF16, kind="Internal").ap()
    x_tiles = x.rearrange("b (t p) d -> p (b t) d", p=P)
    out_tiles = out.rearrange("b (t p) d -> p (b t) d", p=P)

    with ExitStack() as ctx:
        def sb(name, shape, dt=F32):
            return ctx.enter_context(nc.sbuf_tensor(name, shape, dt))

        def ps(name, shape, dt=F32):
            return ctx.enter_context(nc.psum_tensor(name, shape, dt))

        def sem(name):
            return ctx.enter_context(nc.semaphore(name))

        x_flat = sb("x_flat", [P, NT * D])
        x_sb = x_flat[:, :].rearrange("p (n d) -> p n d", d=D)
        wq_sb, wk_sb = sb("wq_sb", [P, D]), sb("wk_sb", [P, D])
        wq_ord, wk_ord = sb("wq_ord", [P, D]), sb("wk_ord", [P, D])
        wqg, wkg = sb("wqg", [P, D]), sb("wkg", [P, D])
        wv_sb = sb("wv_sb", [P, HG])
        bv_sb = sb("bv_sb", [H * G, H])
        wsel = sb("wsel", [P, K, D])
        bsel = sb("bsel", [K, D])
        ids_sb, ids_col = sb("ids_sb", [1, K], I32), sb("ids_col", [K, 1], I32)
        mix_all = sb("mix_all", [P, K])
        mix_col = sb("mix_col", [K, 1])
        mix_rows = sb("mix_rows", [K, P])
        gamma_col, beta_col = sb("gamma_col", [P, 1]), sb("beta_col", [P, 1])
        bq_col, bk_col = sb("bq_col", [P, 1]), sb("bk_col", [P, 1])
        bias_qk = sb("bias_qk", [P, 2])
        ones = sb("ones", [P, P])
        warm = sb("warm", [P, 2])
        zeros = sb("zeros", [P, 2 * S])
        ident = sb("ident", [P, P])
        ident_bf = sb("ident_bf", [P, P], BF16)
        mix_ident = sb("mix_ident", [P, K, P])
        beta_bc = sb("beta_bc", [P, P])
        wv_sum = sb("wv_sum", [P, H * G])
        bv_sum, bv_diag = sb("bv_sum", [H * G, 1]), sb("bv_diag", [H * G, P])
        wv_four, wv_two = sb("wv_four", [P, H * G, H // 2]), sb("wv_two", [P, H * G, H // 4])
        w_vy = sb("w_vy", [P, 2 * D])
        adapter_bias, value_bias = sb("adapter_bias", [P, D]), sb("value_bias", [P, TT, G])
        out_bias = sb("out_bias", [P, TT, D])
        bn = sb("bn", [P, NT, 6])
        mean_var = sb("mean_var", [P, NT * 2])
        var_in, std0, rstd0 = sb("var_in", [P, 2, NT]), sb("std0", [P, 2, NT]), sb("rstd0", [P, 2, NT])
        std, rstd = sb("std", [P, 2, NT]), sb("rstd", [P, 2, NT])
        rstd_flat = rstd[:, :, :].rearrange("p a n -> p (a n)")
        ratio = sb("ratio", [P, NT])
        z = sb("z", [P, RING, TT, D])
        zt_sb = sb("zt_sb", [P, RING, S])
        qk32 = sb("qk32", [P, 2, 2, S])
        rest = sb("rest", [P, 2, S])
        parts = sb("parts", [P, 2, 6, S], BF16)
        stack = sb("stack", [ROWS, RING, 2, H, S], BF16)
        nmax = sb("nmax", [P, 2, H * TT])
        nmax_parts = sb("nmax_parts", [P, 2, 2 * H * TT], BF16)
        nmax_rows = sb("nmax_rows", [2 * H * TT, 2, P], BF16)
        probs = sb("probs", [P, H, TT, S])
        values = sb("values", [P, RING, TT, H, 2 * G])
        adapters = sb("adapters", [P, RING, TT, D])
        att = sb("att", [P, 2, TT, C, 2 * G])
        rden = sb("rden", [P, 2, TT, C])
        normed = sb("normed", [P, 2, TT, D])
        summed = sb("summed", [P, 2, TT, D])
        result = sb("result", [P, 2, TT, D])

        max_ps = [ps(f"max_ps{i}", [P, TT, S]) for i in range(2)]
        exp_ps = [ps(f"exp_ps{i}", [P, TT, S]) for i in range(2)]
        out_ps = ps("out_ps", [P, 2 * S])
        zt_ps = ps("zt_ps", [P, 2 * S])
        qk_ps = ps("qk_ps", [P, 2, S])
        vy_ps = ps("vy_ps", [P, TT, 2 * D])
        nmax_ps = zt_ps[:, S:2 * S].bitcast(BF16)
        bias_ps = exp_ps[0][:, 0, 0:2]
        vbias_ps = exp_ps[0][:, 0, P:2 * P]
        abias_ps = exp_ps[0][:, 1, 0:P]
        adapt_ps = exp_ps[1][:, 0, 0:P]

        x_first, x_second, x_third = sem("x_first"), sem("x_second"), sem("x_third")
        ids_loaded, qk_loaded, wv_loaded = sem("ids_loaded"), sem("qk_loaded"), sem("wv_loaded")
        bias_loaded, bv_loaded = sem("bias_loaded"), sem("bv_loaded")
        mix_loaded, adapters_loaded, abias_loaded = sem("mix_loaded"), sem("adapters_loaded"), sem("abias_loaded")
        ones_ready, ident_ready = sem("ones_ready"), sem("ident_ready")
        pool_setup, dve_setup = sem("pool_setup"), sem("dve_setup")
        var_ready, std_ready = sem("var_ready"), sem("std_ready")
        wqk_ready, bias_ready = sem("wqk_ready"), sem("bias_ready")
        wv_summed = sem("wv_summed")
        bias_in_psum, vbias_ready, mix_ready = sem("bias_in_psum"), sem("vbias_ready"), sem("mix_ready")
        mixed_in_psum, mixed_in_sbuf = sem("mixed_in_psum"), sem("mixed_in_sbuf")
        value_weights_ready, out_bias_ready = sem("value_weights_ready"), sem("out_bias_ready")
        z_ready, zt_in_psum, zt_in_sbuf = sem("z_ready"), sem("zt_in_psum"), sem("zt_in_sbuf")
        qk_in_psum, qk_in_sbuf = sem("qk_in_psum"), sem("qk_in_sbuf")
        split_steps, parts_stored = sem("split_steps"), sem("parts_stored")
        stack_loaded = [sem(f"stack_loaded{i}") for i in range(RING)]
        rows_loaded = [sem(f"rows_loaded{i}") for i in range(RING)]
        max_scores, max_done, nmax_split = sem("max_scores"), sem("max_done"), sem("nmax_split")
        nmax_in_psum, nmax_in_sbuf = sem("nmax_in_psum"), sem("nmax_in_sbuf")
        exp_scores, exp_done, out_in_psum = sem("exp_scores"), sem("exp_done"), sem("out_in_psum")
        vy_in_psum, values_ready, adapters_ready = sem("vy_in_psum"), sem("values_ready"), sem("adapters_ready")
        att_ready, rden_ready, normed_ready = sem("att_ready"), sem("rden_ready"), sem("normed_ready")
        final_steps = sem("final_steps")
        stored = [sem(f"stored{i}") for i in range(2)]

        def steps(engine, step, before=()):
            def one(t, base):
                step(lambda lead: base + (t + lead), lambda lead: (t + lead) % RING,
                     lambda lead: not isinstance(base, int) or 0 <= t + lead < B)

            first = -LAG_OUT
            turns = (B - LEAD_Z - first) // RING
            for t in range(-LEAD_Z, first):
                for work in [w for at, w in before if at == t]:
                    work()
                one(t, 0)
            with engine.Fori(0, turns) as i:
                for t in range(first, first + RING):
                    one(t, i * RING)
            for t in range(first + turns * RING, B - LAG_OUT):
                one(t, 0)

        START = 16
        started = [out_in_psum, final_steps, exp_scores, exp_done, att_ready, *stack_loaded, *rows_loaded, *stored]

        def release(engine, semaphore, value, start=0):
            if not isinstance(value, int) or value > 0:
                engine.wait_ge(semaphore, value + start)

        def pass1_turn(turn):
            return (LEAD_ROWS, turn + HALF) if turn < HALF else (LEAD_MAX, turn - HALF)

        STATS = [(0, TT), (TT, 4 * TT), (4 * TT, NT)]
        LOADS = 3
        ADAPTERS = [(0, 5 * K // 8), (5 * K // 8, 3 * K // 4), (3 * K // 4, K)]

        def load_adapters(engine, lo, hi):
            engine.wait_ge(ids_loaded, 32)
            for k in range(lo, hi):
                which = engine.value_load(ids_sb[0:1, k:k + 1], min_val=0, max_val=N_AD - 1)
                engine.dma_start(wsel[:, k, :], W[bass.ds(which, 1)].rearrange("n o i -> o (n i)"))\
                      .then_inc(adapters_loaded, 16)

        def stack_count(n, s, more):
            return (n - s) * (LOADS * 16 // RING) + more * 16

        block = ctx.enter_context(nc.Block())

        @block.sync
        def _(sp):
            sp.dma_start(x_sb[:, 0:TT, :], x_tiles[:, 0:TT, :]).then_inc(x_first, 16)
            sp.dma_start(wq_sb[:, :], Wq).then_inc(qk_loaded, 16)
            sp.dma_start(gamma_col[:, :], gamma.rearrange("(p a) -> p a", a=1)).then_inc(qk_loaded, 16)
            sp.dma_start(wk_sb[:, :], Wk).then_inc(qk_loaded, 16)
            sp.dma_start(beta_col[:, :], beta.rearrange("(p a) -> p a", a=1)).then_inc(bias_loaded, 16)
            with nc.allow_non_contiguous_dma(reason="two vectors of 128 numbers, reordered"):
                for bias, col in ((bq, bq_col), (bk, bk_col)):
                    sp.dma_start(col[:, :], bias.rearrange("(h k a) -> k h a", k=DK, a=1)).then_inc(bias_loaded, 16)
            sp.dma_start(x_sb[:, TT:4 * TT, :], x_tiles[:, TT:4 * TT, :]).then_inc(x_second, 16)
            sp.dma_start(ids_sb[:, :], ids.rearrange("(a k) -> a k", a=1)).then_inc(ids_loaded, 16)
            sp.dma_start(ids_col[:, :], ids.rearrange("(k a) -> k a", a=1)).then_inc(ids_loaded, 16)
            sp.dma_start(wv_sb[:, :], Wv).then_inc(wv_loaded, 16)
            sp.dma_start(bv_sb[:, :], bv.rearrange("(n j) -> n j", j=H)).then_inc(bv_loaded, 16)
            sp.dma_start(mix_all[:, :], weights.rearrange("(a k) -> a k", a=1).to_broadcast([P, K]))\
              .then_inc(mix_loaded, 16)
            sp.dma_start(mix_col[:, :], weights.rearrange("(k a) -> k a", a=1)).then_inc(mix_loaded, 16)
            sp.dma_start(x_sb[:, 4 * TT:NT, :], x_tiles[:, 4 * TT:NT, :]).then_inc(x_third, 16)

            def step(batch, slot, runs):
                if runs(LEAD_STACK):
                    n, s = batch(LEAD_STACK), slot(LEAD_STACK)
                    release(sp, exp_scores, (n - RING + 1) * H, START)
                    sp.wait_ge(parts_stored, n * 16 + 16)
                    row = 0
                    for count in (3, 2, 1):
                        sp.dma_start(
                            stack[row:row + count * DK, s, :, :, :].rearrange("r a h s -> r a (h s)"),
                            scratch[s, 3 - count:3 + count, :].rearrange("(a r) (k n) -> (r k) a n", a=2, k=DK))\
                          .then_inc(stack_loaded[s], 16)
                        row += count * DK
                if runs(LEAD_ROWS):
                    n, s = batch(LEAD_ROWS), slot(LEAD_ROWS)
                    sp.wait_ge(nmax_in_sbuf, n + 1)
                    sp.dma_start(stack[STACK:ROWS, s, 0, :, :].rearrange("r h s -> r (h s)"),
                                 nmax_rows[:, s % 2, :]).then_inc(rows_loaded[s], 16)
                if runs(LEAD_PROJ):
                    n, s = batch(LEAD_PROJ), slot(LEAD_PROJ)
                    release(sp, stack_loaded[s], stack_count(n, s, 0), START)
                    sp.wait_ge(split_steps, n * 3 + 3)
                    sp.dma_start(scratch[s].rearrange("r (p s) -> p r s", p=P), parts[:, s % 2, :, :])\
                      .then_inc(parts_stored, 16)
                if runs(LAG_OUT):
                    n, s = batch(LAG_OUT), slot(LAG_OUT)
                    sp.wait_ge(final_steps, n * 2 + 2 + START)
                    sp.dma_start(out_tiles[:, bass.ds(n * TT, TT), :], result[:, s % 2, :, :])\
                      .then_inc(stored[s % 2], 16)

            steps(sp, step, before=[(-LEAD_Z, lambda: load_adapters(sp, *ADAPTERS[0])),
                                    (-LEAD_STACK, lambda: load_adapters(sp, *ADAPTERS[1]))])
            for q in stored:
                sp.wait_ge(q, 16 * B // 2 + START)

        @block.gpsimd
        def _(pool):
            pool.memset(ident[:, :], 0.0).then_inc(pool_setup, 1)
            pool.memset(zeros[:, :], 0.0).then_inc(pool_setup, 1)
            pool.wait_ge(pool_setup, 2)
            pool.affine_select(out=ident[:, :], in_=ident[:, :], compare_op=ALU.not_equal, fill=1.0, base=0,
                               pattern=[[-1, P]], channel_multiplier=1).then_inc(ident_ready, 1)
            pool.wait_ge(ident_ready, 1)
            pool.tensor_tensor(ident_bf[:, :], ident[:, :], zeros[:, 0:P], ALU.add).then_inc(ident_ready, 1)

            pool.memset(values[:, :, :, :, G:2 * G], 1.0).then_inc(pool_setup, 1)
            pool.wait_ge(ident_ready, 2)

            def slot_ones(s, batches=0):
                def work():
                    if batches:
                        pool.wait_ge(split_steps, batches * 3)
                    pool.wait_ge(pool_setup, 3 + s)
                    pool.memset(stack[STACK:ROWS, s, 1, :, :], 1.0).then_inc(pool_setup, 1)
                    pool.wait_ge(pool_setup, 4 + s)
                return work

            for s in range(RING - 2):
                slot_ones(s)()

            pool.wait_ge(ids_loaded, 32)
            pool.indirect_dma_start(bsel[:, :], None, b, bass.IndirectOffsetOnAxis(ap=ids_col[:, 0:1], axis=0))\
                .then_inc(abias_loaded, 16)

            def value_weights():
                pool.wait_ge(wv_loaded, 16)
                summand = wv_sb[:, :].rearrange("p (n j) -> p n j", j=H)
                for done, total in enumerate((wv_four[:, :, :], wv_two[:, :, :],
                                              wv_sum[:, :].rearrange("p (n a) -> p n a", a=1))):
                    half = total.shape[2]
                    if done:
                        pool.wait_ge(wv_summed, done)
                    pool.tensor_tensor(total, summand[:, :, 0:half], summand[:, :, half:2 * half], ALU.add)\
                        .then_inc(wv_summed, 1)
                    summand = total

            def output_bias():
                pool.wait_ge(mixed_in_sbuf, 3)
                for t in range(TT):
                    last = pool.tensor_tensor(
                        out_bias[:, t, :].rearrange("p (c g) -> p c g", g=G),
                        adapter_bias[:, :].rearrange("p (c g) -> p c g", g=G),
                        value_bias[:, t:t + 1, :].to_broadcast([P, C, G]), ALU.add)
                last.then_inc(out_bias_ready, 1)

            def step(batch, slot, runs):
                if runs(LEAD_ROWS):
                    n, s = batch(LEAD_ROWS), slot(LEAD_ROWS)
                    nmax_n = nmax[:, s % 2, :]
                    high, low = nmax_parts[:, s % 2, 0:H * TT], nmax_parts[:, s % 2, H * TT:2 * H * TT]
                    pool.wait_ge(max_done, n * H + H)
                    release(pool, nmax_in_psum, n - 1)
                    pool.tensor_tensor(high, nmax_n, zeros[:, 0:H * TT], ALU.add).then_inc(nmax_split, 1)
                    pool.wait_ge(nmax_split, n * 2 + 1)
                    pool.tensor_tensor(low, nmax_n, high, ALU.subtract).then_inc(nmax_split, 1)
                if runs(LEAD_PROJ):
                    n, s = batch(LEAD_PROJ), slot(LEAD_PROJ)
                    qk_n, none = qk32[:, s % 2, :, :], zeros[:, :].rearrange("p (a s) -> p a s", a=2)
                    low, middle, high = parts[:, s % 2, 0:6:5, :], parts[:, s % 2, 1:5:3, :], parts[:, s % 2, 2:4, :]
                    pool.wait_ge(qk_in_sbuf, n * 2 + 2)
                    release(pool, split_steps, n * 3)
                    pool.tensor_tensor(rest[:, :, :], qk_n, high, ALU.subtract).then_inc(split_steps, 1)
                    pool.wait_ge(split_steps, n * 3 + 1)
                    pool.tensor_tensor(middle, rest[:, :, :], none, ALU.add).then_inc(split_steps, 1)
                    pool.wait_ge(split_steps, n * 3 + 2)
                    pool.tensor_tensor(low, rest[:, :, :], middle, ALU.subtract).then_inc(split_steps, 1)
                if runs(LAG_OUT):
                    n, s = batch(LAG_OUT), slot(LAG_OUT)
                    pool.wait_ge(normed_ready, n + 1)
                    pool.wait_ge(final_steps, n * 2 + 1 + START)
                    release(pool, stored[s % 2], (n - s % 2) * 8, START)
                    pool.tensor_tensor(result[:, s % 2, :, :].rearrange("p t d -> p (t d)"),
                                       normed[:, s % 2, :, :].rearrange("p t d -> p (t d)"),
                                       summed[:, s % 2, :, :].rearrange("p t d -> p (t d)"), ALU.add)\
                        .then_inc(final_steps, 1)
                if runs(0):
                    n, s = batch(0), slot(0)
                    pool.wait_ge(adapters_ready, n * TT + TT)
                    release(pool, final_steps, n * 2 - 2, START)
                    pool.tensor_tensor(summed[:, s % 2, :, :].rearrange("p t d -> p (t d)"),
                                       adapters[:, s, :, :].rearrange("p t d -> p (t d)"),
                                       x_flat[:, bass.ds(n * TT * D, TT * D)], ALU.add).then_inc(final_steps, 1)

            steps(pool, step, before=[(-LEAD_STACK, value_weights), (-LEAD_MAX, slot_ones(RING - 2, 2)),
                                      (-LEAD_ROWS, output_bias), (0, slot_ones(RING - 1, LEAD_PROJ))])

        @block.scalar
        def _(act):
            act.wait_ge(ones_ready, 1)
            nc.scalar.activation(warm[:, 0:1], ones[:, 0:1], ACT.Sqrt)

            def roots(group):
                lo, hi = STATS[group]
                act.wait_ge(var_ready, 2 * group + 2)
                nc.scalar.activation(std0[:, :, lo:hi], var_in[:, :, lo:hi], ACT.Sqrt).then_inc(std_ready, 1)

            def diagonals(lo, hi):
                for k in range(lo, hi):
                    nc.scalar.activation(mix_ident[:, k, :], ident[:, :], ACT.Copy, scale=mix_all[:, k:k + 1])\
                        .then_inc(mix_ready, 1)

            def mixed():
                roots(2)
                nc.scalar.activation(warm[:, 1:2], ones[:, 0:1], ACT.Exp)
                act.wait_ge(mixed_in_psum, 1)
                nc.scalar.activation(w_vy[:, D:2 * D], adapt_ps, ACT.Copy).then_inc(mixed_in_sbuf, 1)
                nc.scalar.activation(adapter_bias[:, :], abias_ps, ACT.Copy).then_inc(mixed_in_sbuf, 1)
                for t in range(TT):
                    for j in range(HALF):
                        q, head = slice(A * j, A * j + A), (t * HALF + j) * G
                        last = nc.scalar.activation(value_bias[q, t, :], vbias_ps[q, head:head + G], ACT.Copy)
                last.then_inc(mixed_in_sbuf, 1)

            def second():
                roots(1)
                load_adapters(act, *ADAPTERS[2])
                act.wait_ge(mix_loaded, 32)
                act.wait_ge(ident_ready, 1)
                diagonals(0, K // 2)

            set_up = {0: second, 2: mixed}

            def step(batch, slot, runs):
                def exponentials(*heads):
                    for u in heads if runs(0) else ():
                        n = batch(0)
                        act.wait_ge(exp_scores, n * H + u + 1 + START)
                        if u % HALF == 0:
                            release(act, out_in_psum, n * 2 + (u // HALF - 1), START)
                        nc.scalar.activation(probs[:, u, :, :], exp_ps[u % 2][:, :, :], ACT.Exp, scale=SCALE)\
                          .then_inc(exp_done, 1)

                def tokens():
                    if runs(LEAD_Z):
                        n, s = batch(LEAD_Z), slot(LEAD_Z)
                        act.wait_ge(zt_in_psum, n + 1)
                        release(act, vy_in_psum, n - RING + 1)
                        nc.scalar.activation(zt_sb[:, s, :], zt_ps[:, 0:S], ACT.Copy).then_inc(zt_in_sbuf, 1)

                def queries_keys(side):
                    if runs(LEAD_PROJ):
                        n, s = batch(LEAD_PROJ), slot(LEAD_PROJ)
                        if side == 0:
                            act.wait_ge(qk_in_psum, n + 1)
                            release(act, split_steps, (n - 2) * 3 + 1)
                            release(act, parts_stored, (n - 1) * 16)
                            if isinstance(n, int) and n == 0:
                                act.wait_ge(bias_ready, 1)
                        bias = bias_qk[:, side:side + 1]
                        nc.scalar.activation(qk32[:, s % 2, side, :], qk_ps[:, side, :], ACT.Identity, bias=bias)
                        nc.scalar.activation(parts[:, s % 2, 2 + side, :], qk_ps[:, side, :], ACT.Identity,
                                             bias=bias).then_inc(qk_in_sbuf, 1)

                def maxima():
                    if runs(LEAD_ROWS):
                        n, s = batch(LEAD_ROWS), slot(LEAD_ROWS)
                        act.wait_ge(nmax_in_psum, n + 1)
                        if not isinstance(n, int) or n >= 2:
                            before = (s - 2) % RING
                            act.wait_ge(rows_loaded[before],
                                        n * (16 // RING) + (16 - (2 + before) * (16 // RING) + START))
                        nc.scalar.activation(nmax_rows[:, s % 2, :], nmax_ps[0:2 * H * TT, 0:P], ACT.Copy)\
                          .then_inc(nmax_in_sbuf, 1)

                def value_columns():
                    if runs(LEAD_ROWS):
                        n, s = batch(LEAD_ROWS), slot(LEAD_ROWS)
                        act.wait_ge(vy_in_psum, n + 1)
                        release(act, out_in_psum, n * 2 - 2 * (RING - 1), START)
                        for t in range(TT):
                            last = nc.scalar.activation(values[:, s, t, :, 0:G],
                                                        vy_ps[:, t, 0:D].rearrange("p (h g) -> p h g", g=G), ACT.Copy)
                        last.then_inc(values_ready, 1)

                queries_keys(0)
                exponentials(0)
                queries_keys(1)
                if not runs(0) and batch(LEAD_PROJ) in set_up:
                    set_up[batch(LEAD_PROJ)]()
                exponentials(1, 2, 3)
                maxima()
                value_columns()
                exponentials(4, 5)
                tokens()
                exponentials(6, 7)

            steps(act, step, before=[(-LEAD_Z, lambda: roots(0)), (-LEAD_MAX, lambda: diagonals(K // 2, K))])

        @block.vector
        def _(dve):
            done = [0]

            def link(ins):
                done[0] += 1
                ins.then_inc(dve_setup, 1)
                dve.wait_ge(dve_setup, done[0])

            mv = mean_var[:, :].rearrange("p (n a) -> p n a", a=2)

            def statistics(group):
                lo, hi = STATS[group]
                dve.wait_ge((x_first, x_second, x_third)[group], 16)
                for n in range(lo, hi):
                    last = nc.vector.bn_stats(bn[:, n, :], x_sb[:, n, :])
                link(last)
                for n in range(lo, hi):
                    last = nc.vector.bn_aggr(mv[:, n, :], bn[:, n, :])
                link(last)
                nc.vector.tensor_scalar(var_in[:, 0, lo:hi], mv[:, lo:hi, 1], EPS, None, ALU.add).then_inc(var_ready, 1)
                nc.vector.tensor_scalar(var_in[:, 1, lo:hi], mv[:, lo:hi, 1], 1.0 + EPS, EPS * EPS,
                                        ALU.mult, ALU.add).then_inc(var_ready, 1)

            def deviations(group):
                lo, hi = STATS[group]
                v, s0, r0 = var_in[:, :, lo:hi], std0[:, :, lo:hi], rstd0[:, :, lo:hi]
                s1, r1 = std[:, :, lo:hi], rstd[:, :, lo:hi]
                dve.wait_ge(std_ready, group + 1)
                link(nc.vector.reciprocal(r0, s0))
                link(nc.vector.tensor_tensor(s1, v, r0, ALU.mult))
                link(nc.vector.tensor_tensor(s1, s1, s0, ALU.add))
                link(nc.vector.tensor_scalar(s1, s1, 0.5, None, ALU.mult))
                link(nc.vector.reciprocal(r1, s1))
                link(nc.vector.tensor_tensor(ratio[:, lo:hi], std[:, 1, lo:hi], rstd[:, 0, lo:hi], ALU.mult))

            def first():
                nc.vector.memset(ones[:, :], 1.0).then_inc(ones_ready, 1)
                statistics(0)
                deviations(0)

            def second():
                dve.wait_ge(qk_loaded, 48)
                for w, ordered, scaled in ((wq_sb, wq_ord, wqg), (wk_sb, wk_ord, wkg)):
                    by_column = w[:, :].rearrange("p (h k) -> p k h", k=DK)
                    nc.vector.tensor_copy(ordered[:, :].rearrange("p (k h) -> p k h", k=DK), by_column)
                    nc.vector.tensor_scalar(scaled[:, :].rearrange("p (k h) -> p k h", k=DK), by_column,
                                            gamma_col[:, :], None, ALU.mult).then_inc(wqk_ready, 1)
                dve.wait_ge(bias_in_psum, 1)
                dve.wait_ge(bias_loaded, 48)
                nc.vector.tensor_tensor(bias_qk[:, 0:1], bias_ps[:, 0:1], bq_col[:, :], ALU.add)
                nc.vector.tensor_tensor(bias_qk[:, 1:2], bias_ps[:, 1:2], bk_col[:, :], ALU.add).then_inc(bias_ready, 1)
                statistics(1)
                deviations(1)

            def third():
                dve.wait_ge(bv_loaded, 16)
                link(nc.vector.tensor_reduce(bv_sum[:, :], bv_sb[:, :], AX.X, ALU.add))
                dve.wait_ge(ident_ready, 1)
                nc.vector.tensor_scalar(bv_diag[:, :], ident[:, :], bv_sum[:, :], None, ALU.mult)
                nc.vector.tensor_scalar(beta_bc[:, :], ones[:, :], beta_col[:, :], None, ALU.mult)
                dve.wait_ge(mix_loaded, 32)
                nc.vector.tensor_scalar(mix_rows[:, :], ones[0:K, :], mix_col[:, :], None, ALU.mult)\
                    .then_inc(vbias_ready, 1)
                statistics(2)
                dve.wait_ge(wv_summed, 3)
                nc.vector.tensor_scalar(w_vy[:, 0:D], wv_sum[:, :], gamma_col[:, :], None, ALU.mult)\
                    .then_inc(value_weights_ready, 1)

            def step(batch, slot, runs):
                def maxima(*turns):
                    for lead, u in map(pass1_turn, turns):
                        if runs(lead):
                            n, s = batch(lead), slot(lead)
                            if u == 0:
                                release(dve, nmax_split, (n - 1) * 2)
                            dve.wait_ge(max_scores, n * H + u + 1)
                            nc.vector.tensor_reduce(nmax[:, s % 2, u * TT:(u + 1) * TT], max_ps[u % 2][:, :, :], AX.X,
                                                    ALU.max, negate=True).then_inc(max_done, 1)

                def mixture(t):
                    n, s = batch(LEAD_ROWS), slot(LEAD_ROWS)
                    if runs(LEAD_ROWS):
                        if isinstance(n, int) and n == 0:
                            dve.wait_ge(out_bias_ready, 1)
                        if t == 0:
                            dve.wait_ge(values_ready, n + 1)
                            release(dve, final_steps, n * 2 - (2 * RING - 1), START)
                        nc.vector.scalar_tensor_tensor(adapters[:, s, t, :], vy_ps[:, t, D:2 * D],
                                                       ratio[:, bass.ds(n * TT + t, 1)], out_bias[:, t, :],
                                                       ALU.mult, ALU.add).then_inc(adapters_ready, 1)

                def normalized():
                    n, s = batch(LEAD_Z), slot(LEAD_Z)
                    if runs(LEAD_Z):
                        release(dve, zt_in_psum, n - RING + 1)
                    for t in range(TT) if runs(LEAD_Z) else ():
                        tile = n * TT + t
                        nc.vector.tensor_scalar(z[:, s, t, :], x_flat[:, bass.ds(tile * D, D)],
                                                mean_var[:, bass.ds(tile * 2, 1)], rstd_flat[:, bass.ds(tile + NT, 1)],
                                                ALU.subtract, ALU.mult).then_inc(z_ready, 1)

                o, s = batch(LAG_OUT), slot(LAG_OUT)
                att_o, rden_o = att[:, s % 2, :, :, :], rden[:, s % 2, :, :]
                maxima(0)
                normalized()
                maxima(1, 2, 3)
                if runs(LAG_OUT):
                    dve.wait_ge(out_in_psum, o * 2 + 2 + START)
                    nc.vector.transpose(att_o.rearrange("p t c g -> p (t c) g"),
                                        out_ps[:, :].rearrange("p (t a c) -> p t c a", t=TT, c=C))\
                        .then_inc(att_ready, 1)
                maxima(4)
                if runs(LAG_OUT):
                    dve.wait_ge(att_ready, o + 1 + START)
                    nc.vector.reciprocal(rden_o, att_o[:, :, :, G]).then_inc(rden_ready, 1)
                maxima(5)
                if runs(LAG_OUT):
                    dve.wait_ge(rden_ready, o + 1)
                    release(dve, final_steps, o * 2 - 2, START)
                    nc.vector.tensor_tensor(
                        normed[:, s % 2, :, :].rearrange("p t (c g) -> p (t c) g", g=G),
                        att_o.rearrange("p t c g -> p (t c) g")[:, :, 0:G],
                        rden_o.rearrange("p t (c a) -> p (t c) a", a=1).to_broadcast([P, TT * C, G]),
                        ALU.mult).then_inc(normed_ready, 1)
                maxima(6)
                mixture(0)
                mixture(1)
                maxima(7)

            steps(dve, step, before=[(-LEAD_Z, first), (-LEAD_Z + 1, second), (-LEAD_MAX, third),
                                      (-LEAD_ROWS, lambda: deviations(2))])

        @block.tensor
        def _(pe):
            for q in started:
                pe.sem_inc(q, START)
            pe.wait_ge(ident_ready, 2)

            def keep_warm(count):
                for _ in range(count):
                    nc.tensor.matmul(out_ps[:, :], ident_bf[:, :], zeros[:, 0:S].bitcast(BF16), start=True, stop=True,
                                     skip_group_check=True)

            keep_warm(9)

            def biases():
                pe.wait_ge(wqk_ready, 2)
                pe.wait_ge(bias_loaded, 48)
                nc.tensor.matmul(bias_ps[:, 0:1], wq_ord[:, :], beta_col[:, :], start=True, stop=True)
                nc.tensor.matmul(bias_ps[:, 1:2], wk_ord[:, :], beta_col[:, :], start=True, stop=True)\
                  .then_inc(bias_in_psum, 1)

            def mixing():
                pe.wait_ge(bias_ready, 1)
                pe.wait_ge(vbias_ready, 1)
                pe.wait_ge(wv_summed, 3)
                nc.tensor.matmul(vbias_ps, beta_bc[:, :], wv_sum[:, :], start=True, stop=False)
                nc.tensor.matmul(vbias_ps, ones[:, :], bv_diag[:, :], start=False, stop=True)
                pe.wait_ge(abias_loaded, 16)
                nc.tensor.matmul(abias_ps, mix_rows[:, :], bsel[:, :], start=True, stop=True)
                pe.wait_ge(mix_ready, K)
                pe.wait_ge(adapters_loaded, 16 * K)
                for k in range(K):
                    last = nc.tensor.matmul(adapt_ps, wsel[:, k, :], mix_ident[:, k, :],
                                            start=(k == 0), stop=(k == K - 1))
                last.then_inc(mixed_in_psum, 1)

            def step(batch, slot, runs):
                filling = not runs(0) and runs(LEAD_PROJ)
                draining = not runs(LEAD_ROWS)

                def pass1(turn):
                    lead, u = pass1_turn(turn)
                    if runs(lead):
                        n, s = batch(lead), slot(lead)
                        if u == 0:
                            pe.wait_ge(stack_loaded[s], stack_count(n, s, LOADS) + START)
                        release(pe, max_done, n * H + u - 1)
                        if filling:
                            keep_warm(1)
                        for t in range(TT):
                            last = nc.tensor.matmul(max_ps[u % 2][:, t, :], stack[0:STACK, s, 0, u, t * P:(t + 1) * P],
                                                    stack[0:STACK, s, 1, u, :], start=True, stop=True)
                        last.then_inc(max_scores, 1)

                def pass2(u):
                    if runs(0):
                        n, s = batch(0), slot(0)
                        if u == 0:
                            pe.wait_ge(rows_loaded[s], (n - s) * (16 // RING) + 16 + START)
                            if isinstance(n, int) and n == 0:
                                pe.wait_ge(pool_setup, 4)
                        release(pe, exp_done, n * H + u - 1, START)
                        for t in range(TT):
                            last = nc.tensor.matmul(exp_ps[u % 2][:, t, :], stack[:, s, 1, u, t * P:(t + 1) * P],
                                                    stack[:, s, 0, u, :], start=True, stop=True)
                        last.then_inc(exp_scores, 1)

                def product(lead, group, t):
                    if runs(lead):
                        n, s = batch(lead), slot(lead)
                        if t == 0:
                            pe.wait_ge(exp_done, n * H + (group + 1) * HALF + START)
                        if group == 0 and t == 0:
                            pe.wait_ge(values_ready, n + 1)
                            release(pe, att_ready, n, START)
                        for j in range(HALF):
                            u = group * HALF + j
                            last = nc.tensor.matmul(out_ps[j * A:(j + 1) * A, group * S:(group + 1) * S],
                                                    values[:, s, t, u, :], probs[:, u, t, :],
                                                    start=(t == 0), stop=(t == TT - 1), skip_group_check=True)
                        if t == TT - 1:
                            last.then_inc(out_in_psum, 1)

                def transposes():
                    if runs(LEAD_Z):
                        n, s = batch(LEAD_Z), slot(LEAD_Z)
                        pe.wait_ge(z_ready, n * TT + TT)
                        release(pe, zt_in_sbuf, n)
                        release(pe, nmax_in_sbuf, n - RING + 1)
                        for t in range(TT):
                            last = nc.tensor.transpose(zt_ps[:, t * P:(t + 1) * P], z[:, s, t, :], ident[:, :])
                        last.then_inc(zt_in_psum, 1)

                def maxima():
                    if runs(LEAD_ROWS):
                        n, s = batch(LEAD_ROWS), slot(LEAD_ROWS)
                        pe.wait_ge(nmax_split, n * 2 + 2)
                        if isinstance(n, int):
                            pe.wait_ge(zt_in_sbuf, min(n + LEAD_PROJ - LEAD_ROWS + 1, B))
                        else:
                            pe.wait_ge(zt_in_sbuf, n + (LEAD_PROJ - LEAD_ROWS + 1))
                        nc.tensor.transpose(nmax_ps[0:2 * H * TT, 0:P], nmax_parts[:, s % 2, :], ident_bf[:, :])\
                          .then_inc(nmax_in_psum, 1)

                def queries_keys():
                    if runs(LEAD_PROJ):
                        n, s = batch(LEAD_PROJ), slot(LEAD_PROJ)
                        pe.wait_ge(zt_in_sbuf, n + 1)
                        release(pe, qk_in_sbuf, n * 2)
                        for side, w in enumerate((wqg, wkg)):
                            last = nc.tensor.matmul(qk_ps[:, side, :], w[:, :], zt_sb[:, s, :], start=True, stop=True)
                        last.then_inc(qk_in_psum, 1)

                def values_adapters():
                    if runs(LEAD_ROWS):
                        n, s = batch(LEAD_ROWS), slot(LEAD_ROWS)
                        if isinstance(n, int) and n == 0:
                            pe.wait_ge(value_weights_ready, 1)
                            pe.wait_ge(mixed_in_sbuf, 3)
                        release(pe, adapters_ready, n * TT)
                        for t in range(TT):
                            last = nc.tensor.matmul(vy_ps[:, t, :], zt_sb[:, s, t * P:(t + 1) * P], w_vy[:, :],
                                                    start=True, stop=True)
                        last.then_inc(vy_in_psum, 1)

                if filling:
                    queries_keys()
                    if batch(LEAD_PROJ) == 0:
                        keep_warm(18)
                    if batch(LEAD_MAX) == 0:
                        mixing()
                pass1(0)
                if not filling:
                    queries_keys()
                pass1(1), pass2(0)
                if draining:
                    pass2(1)
                product(LAG_OUT, 1, 0)
                pass1(2)
                product(LAG_OUT, 1, 1)
                pass1(3)
                if not draining:
                    pass2(1)
                pass2(2)
                pass1(4)
                values_adapters()
                pass2(3)
                pass1(5), pass2(4)
                maxima()
                pass1(6), pass2(5)
                product(0, 0, 0)
                pass1(7)
                transposes()
                pass2(6)
                product(0, 0, 1)
                pass2(7)

            steps(pe, step, before=[(-LEAD_PROJ, biases)])
    return nc


_INS = ['L0_attn_x', 'L0_attn_Wq', 'L0_attn_bq', 'L0_attn_Wk', 'L0_attn_bk', 'L0_attn_Wv', 'L0_attn_bv',
        'L0_attn_gamma', 'L0_attn_beta', 'L0_ffn_W', 'L0_ffn_b', 'L0_ffn_ids', 'L0_ffn_weights']
_OUTS = [((16, 256, 128), 'float32')]


def kernel(**inputs):
    import numpy as _np
    import concourse.bacc as _bacc
    from concourse import mybir as _mybir
    from concourse.bass_utils import run_bass_kernel_spmd as _run

    nc = _bacc.Bacc("TRN2", target_bir_lowering=False, num_devices=1)
    arrays, args = {}, []
    for name in _INS:
        a = _np.ascontiguousarray(inputs[name])
        arrays[f"in_{name}_dram"] = a
        args.append(nc.dram_tensor(f"in_{name}_dram", a.shape, _mybir.dt.from_np(a.dtype), kind="ExternalInput").ap())
    for i, (shape, dtype) in enumerate(_OUTS):
        dt = _mybir.dt.from_np(_np.dtype(dtype))
        args.append(nc.dram_tensor(f"out_{i}_dram", shape, dt, kind="ExternalOutput").ap())
    build(nc, *args)
    r = _run(nc, [arrays], core_ids=[0])
    return r.results[0]["out_0_dram"]
```
